# Optimizing a Trainium2 kernel written in Bass

```python
import numpy as np
import jax
import jax.numpy as jnp

def _softmax(x, axis=-1):
    return jax.nn.softmax(x, axis=axis)

def _gelu(x):
    return jax.nn.gelu(x, approximate=True)

def _silu(x):
    return jax.nn.silu(x)

def _sigmoid(x):
    return jax.nn.sigmoid(x)

def _layernorm(x, axis=-1, eps=1e-05):
    m = jnp.mean(x, axis=axis, keepdims=True)
    v = jnp.var(x, axis=axis, keepdims=True)
    return (x - m) / jnp.sqrt(v + eps)

def _scatter_add(tgt, idx, src, axis=0):
    return tgt.at[idx].add(src)

def _segment_sum(src, seg, n):
    return jax.ops.segment_sum(src, seg, n)
kernel_name = 'mk_adaln_attn_ffn_d1_seqx_r8_0429c1'

def setup_inputs(seed: int=0):
    np.random.seed(seed)
    _w = jnp.asarray

    def _rec_inputs():
        import jax
        import jax.numpy as jnp
        _rk = jax.random.key(seed)
        x = -0.000125 + 0.9999 * jax.random.normal(jax.random.fold_in(_rk, 1), (8, 128, 256), jnp.float32)
        _lenS = 128 - jax.random.randint(jax.random.fold_in(_rk, 7), (8,), 0, max(1, 128 // 4) + 1, jnp.int32)
        _lenS2 = 128 - jax.random.randint(jax.random.fold_in(_rk, 8), (8,), 0, max(1, 128 // 4) + 1, jnp.int32)
        cond_2048 = 7.82532e-05 + 0.0100527 * jax.random.normal(jax.random.fold_in(_rk, 11), (8, 256), jnp.float32)
        return (x, cond_2048)
    x, cond_2048 = _rec_inputs()

    def _L0_cond_setup():
        import jax, jax.numpy as jnp
        import numpy as np
        NUM_BLOCKS = 8
        NUM_LAYERS = 4
        EPS = 1e-06
        key = jax.random.key(seed)
        ks = jax.random.split(key, 6)
        B, S, H = (4, 512, 256)
        inputs = jax.random.normal(ks[0], (B, S, H), dtype=jnp.float32)
        query_vectors = jax.random.normal(ks[1], (NUM_LAYERS, H), dtype=jnp.float32) * 0.01
        lim = float(np.sqrt(6.0 / (H + H)))
        Wk = jax.random.uniform(ks[2], (H, H), minval=-lim, maxval=lim, dtype=jnp.float32)
        Wo = jax.random.uniform(ks[3], (H, H), minval=-lim, maxval=lim, dtype=jnp.float32)
        rms_weight = jnp.ones((H,), dtype=jnp.float32)
        ln_gamma = jnp.ones((H,), dtype=jnp.float32)
        ln_beta = jnp.zeros((H,), dtype=jnp.float32)
        return {'inputs': inputs, 'layer_idx': 1, 'rms_weight': rms_weight, 'query_vectors': query_vectors, 'Wk': Wk, 'Wo': Wo, 'ln_gamma': ln_gamma, 'ln_beta': ln_beta}
    _L0_cond_all = _L0_cond_setup()
    _L0_cond_in = {k: v for k, v in _L0_cond_all.items() if k in ('rms_weight', 'Wk', 'Wo', 'ln_gamma', 'ln_beta')}
    del _L0_cond_all

    def _L0_attn_setup():
        import jax, jax.numpy as jnp
        import numpy as np
        B, T, D = (2, 256, 256)
        H, HD = (16, 128)
        HHD = HD // 2
        SCALE = 1.0 / np.sqrt(HHD).astype(np.float32)
        key = jax.random.key(seed)
        ks = jax.random.split(key, 6)
        s = 1.0 / np.sqrt(D).astype(np.float32)
        return {'x': jax.random.normal(ks[0], (B, T, D), jnp.float32), 'Wq': jax.random.normal(ks[1], (D, H * HD), jnp.float32) * s, 'Wk': jax.random.normal(ks[2], (D, H * HD), jnp.float32) * s, 'Wv': jax.random.normal(ks[3], (D, H * HD), jnp.float32) * s, 'Wo': jax.random.normal(ks[4], (H * HD, D), jnp.float32) * s, 'lambda_init': jnp.full((H,), -0.2, jnp.float32)}
    _L0_attn_all = _L0_attn_setup()
    _L0_attn_in = {k: v for k, v in _L0_attn_all.items() if k in ('Wq', 'Wk', 'Wv', 'Wo', 'lambda_init')}
    del _L0_attn_all

    def _L0_cond2_setup():
        import jax, jax.numpy as jnp
        import numpy as np
        B, T, D = (16, 128, 256)
        key = jax.random.key(seed)
        k0, k1, k2, k3 = jax.random.split(key, 4)
        scale = 1.0 / np.sqrt(D)
        return {'initial_state': jax.random.normal(k0, (B, D), jnp.float32), 'inputs': jax.random.normal(k1, (B, T, D), jnp.float32), 'W_ih': jax.random.normal(k2, (D, 3 * D), jnp.float32) * scale, 'W_hh': jax.random.normal(k3, (D, 3 * D), jnp.float32) * scale, 'b_ih': jnp.zeros((3 * D,), jnp.float32), 'b_hh': jnp.zeros((3 * D,), jnp.float32)}
    _L0_cond2_all = _L0_cond2_setup()
    _L0_cond2_in = {k: v for k, v in _L0_cond2_all.items() if k in ('W_ih', 'W_hh', 'b_ih', 'b_hh')}
    del _L0_cond2_all

    def _L0_ffn_setup():
        import jax, jax.numpy as jnp
        import numpy as np
        BLOCK_SIZE = 32
        HIDDEN_SIZE = 256
        MLP_DIM = 2048
        NVFP4_LUT = jnp.array([0.0, 0.5, 1.0, 1.5, 2.0, 3.0, 4.0, 6.0, 0.0, -0.5, -1.0, -1.5, -2.0, -3.0, -4.0, -6.0], dtype=jnp.float32)

        def dequant_nvfp4(W_packed, scales, block=BLOCK_SIZE):
            N = W_packed.shape[0]
            low = W_packed & 15
            high = W_packed >> 4 & 15
            idx = jnp.stack([low, high], axis=-1).reshape(N, -1)
            vals = NVFP4_LUT[idx]
            K = vals.shape[1]
            vals = vals.reshape(N, K // block, block) * scales[:, :, None]
            return vals.reshape(N, K)
        key = jax.random.key(seed)
        ks = jax.random.split(key, 7)
        x = jax.random.normal(ks[0], (4, 32, HIDDEN_SIZE), dtype=jnp.float32)
        gate_W_packed = jax.random.randint(ks[1], (MLP_DIM, HIDDEN_SIZE // 2), 0, 32, dtype=jnp.int32)
        gate_scales = jax.random.uniform(ks[2], (MLP_DIM, HIDDEN_SIZE // BLOCK_SIZE), dtype=jnp.float32) * 0.1 + 0.001
        up_W_packed = jax.random.randint(ks[3], (MLP_DIM, HIDDEN_SIZE // 2), 0, 32, dtype=jnp.int32)
        up_scales = jax.random.uniform(ks[4], (MLP_DIM, HIDDEN_SIZE // BLOCK_SIZE), dtype=jnp.float32) * 0.1 + 0.001
        down_W_packed = jax.random.randint(ks[5], (HIDDEN_SIZE, MLP_DIM // 2), 0, 32, dtype=jnp.int32)
        down_scales = jax.random.uniform(ks[6], (HIDDEN_SIZE, MLP_DIM // BLOCK_SIZE), dtype=jnp.float32) * 0.1 + 0.001
        return {'x': x, 'gate_W_packed': gate_W_packed, 'gate_scales': gate_scales, 'up_W_packed': up_W_packed, 'up_scales': up_scales, 'down_W_packed': down_W_packed, 'down_scales': down_scales}
    _L0_ffn_all = _L0_ffn_setup()
    _L0_ffn_in = {k: v for k, v in _L0_ffn_all.items() if k in ('gate_W_packed', 'gate_scales', 'up_W_packed', 'up_scales', 'down_W_packed', 'down_scales')}
    del _L0_ffn_all
    return {'x': x, 'cond_2048': cond_2048, 'L0_cond_rms_weight': _L0_cond_in['rms_weight'], 'L0_cond_Wk': _L0_cond_in['Wk'], 'L0_cond_Wo': _L0_cond_in['Wo'], 'L0_cond_ln_gamma': _L0_cond_in['ln_gamma'], 'L0_cond_ln_beta': _L0_cond_in['ln_beta'], 'L0_attn_Wq': _L0_attn_in['Wq'], 'L0_attn_Wk': _L0_attn_in['Wk'], 'L0_attn_Wv': _L0_attn_in['Wv'], 'L0_attn_Wo': _L0_attn_in['Wo'], 'L0_attn_lambda_init': _L0_attn_in['lambda_init'], 'L0_cond2_W_ih': _L0_cond2_in['W_ih'], 'L0_cond2_W_hh': _L0_cond2_in['W_hh'], 'L0_cond2_b_ih': _L0_cond2_in['b_ih'], 'L0_cond2_b_hh': _L0_cond2_in['b_hh'], 'L0_ffn_gate_W_packed': _L0_ffn_in['gate_W_packed'], 'L0_ffn_gate_scales': _L0_ffn_in['gate_scales'], 'L0_ffn_up_W_packed': _L0_ffn_in['up_W_packed'], 'L0_ffn_up_scales': _L0_ffn_in['up_scales'], 'L0_ffn_down_W_packed': _L0_ffn_in['down_W_packed'], 'L0_ffn_down_scales': _L0_ffn_in['down_scales']}

def reference(x, cond_2048, L0_cond_rms_weight, L0_cond_Wk, L0_cond_Wo, L0_cond_ln_gamma, L0_cond_ln_beta, L0_attn_Wq, L0_attn_Wk, L0_attn_Wv, L0_attn_Wo, L0_attn_lambda_init, L0_cond2_W_ih, L0_cond2_W_hh, L0_cond2_b_ih, L0_cond2_b_hh, L0_ffn_gate_W_packed, L0_ffn_gate_scales, L0_ffn_up_W_packed, L0_ffn_up_scales, L0_ffn_down_W_packed, L0_ffn_down_scales):
    import jax
    import jax.numpy as jnp

    def _L0_cond_ref(inputs, layer_idx, rms_weight, query_vectors, Wk, Wo, ln_gamma, ln_beta):
        import jax, jax.numpy as jnp
        import numpy as np
        NUM_BLOCKS = 8
        NUM_LAYERS = 4
        EPS = 1e-06
        B, S, H = inputs.shape
        block_size = max(1, S // NUM_BLOCKS)
        n_blocks = S // block_size
        block_repr = inputs.reshape(B, n_blocks, block_size, H).sum(axis=2)
        keys = jnp.einsum('bnh,kh->bnk', block_repr, Wk)
        rms = jnp.sqrt(jnp.mean(keys * keys, axis=-1, keepdims=True) + EPS)
        keys = keys / rms * rms_weight
        q = query_vectors[layer_idx]
        scores = jnp.einsum('bnh,h->bn', keys, q)
        attn = jax.nn.softmax(scores, axis=-1)
        attended = jnp.einsum('bn,bnh->bh', attn, block_repr)
        attended = jnp.broadcast_to(attended[:, None, :], (B, S, H))
        proj = jnp.einsum('bsh,kh->bsk', attended, Wo)
        x = inputs + proj
        mu = jnp.mean(x, axis=-1, keepdims=True)
        var = jnp.mean((x - mu) ** 2, axis=-1, keepdims=True)
        out = (x - mu) / jnp.sqrt(var + EPS) * ln_gamma + ln_beta
        return out

    def _L0_attn_ref(x, Wq, Wk, Wv, Wo, lambda_init):
        import jax, jax.numpy as jnp
        import numpy as np
        B, T, D = (2, 256, 256)
        H, HD = (16, 128)
        HHD = HD // 2
        SCALE = 1.0 / np.sqrt(HHD).astype(np.float32)
        b, t, d = x.shape
        q = (x @ Wq).reshape(b, t, H, HD).transpose(0, 2, 1, 3)
        k = (x @ Wk).reshape(b, t, H, HD).transpose(0, 2, 1, 3)
        v = (x @ Wv).reshape(b, t, H, HD).transpose(0, 2, 1, 3)
        q1, q2 = (q[..., :HHD], q[..., HHD:])
        k1, k2 = (k[..., :HHD], k[..., HHD:])
        scores1 = jnp.einsum('bhtc,bhsc->bhts', q1, k1) * SCALE
        scores2 = jnp.einsum('bhtc,bhsc->bhts', q2, k2) * SCALE
        causal = jnp.tril(jnp.ones((t, t), bool))
        neg_inf = jnp.float32(-jnp.inf)
        scores1 = jnp.where(causal[None, None], scores1, neg_inf)
        scores2 = jnp.where(causal[None, None], scores2, neg_inf)
        attn1 = jax.nn.softmax(scores1, axis=-1)
        attn2 = jax.nn.softmax(scores2, axis=-1)
        lam = jax.nn.sigmoid(lambda_init)[None, :, None, None]
        diff_attn = attn1 - lam * attn2
        out = jnp.einsum('bhts,bhsd->bhtd', diff_attn, v)
        out = out.transpose(0, 2, 1, 3).reshape(b, t, H * HD)
        return out @ Wo

    def _L0_cond2_ref(initial_state, inputs, W_ih, W_hh, b_ih, b_hh):
        import jax, jax.numpy as jnp
        import numpy as np
        B, T, D = (16, 128, 256)
        "ScanOverTime(GRU cell): sequential per-timestep module call with\n            dict-state passing; merge_dict_trees stacks the per-step\n            'state_predicted' tensors along axis=1 -> [B, T, D]."

        def cell(h, x):
            gi = x @ W_ih + b_ih
            gh = h @ W_hh + b_hh
            i_r, i_z, i_n = jnp.split(gi, 3, axis=-1)
            h_r, h_z, h_n = jnp.split(gh, 3, axis=-1)
            r = jax.nn.sigmoid(i_r + h_r)
            z = jax.nn.sigmoid(i_z + h_z)
            n = jnp.tanh(i_n + r * h_n)
            h_new = (1.0 - z) * n + z * h
            return (h_new, h_new)
        xs = jnp.swapaxes(inputs, 0, 1)
        _, hs = jax.lax.scan(cell, initial_state, xs)
        return jnp.swapaxes(hs, 0, 1)

    def _L0_ffn_ref(x, gate_W_packed, gate_scales, up_W_packed, up_scales, down_W_packed, down_scales):
        import jax, jax.numpy as jnp
        import numpy as np
        BLOCK_SIZE = 32
        HIDDEN_SIZE = 256
        MLP_DIM = 2048
        NVFP4_LUT = jnp.array([0.0, 0.5, 1.0, 1.5, 2.0, 3.0, 4.0, 6.0, 0.0, -0.5, -1.0, -1.5, -2.0, -3.0, -4.0, -6.0], dtype=jnp.float32)

        def dequant_nvfp4(W_packed, scales, block=BLOCK_SIZE):
            N = W_packed.shape[0]
            low = W_packed & 15
            high = W_packed >> 4 & 15
            idx = jnp.stack([low, high], axis=-1).reshape(N, -1)
            vals = NVFP4_LUT[idx]
            K = vals.shape[1]
            vals = vals.reshape(N, K // block, block) * scales[:, :, None]
            return vals.reshape(N, K)
        B, S, H = x.shape
        xt = x.reshape(B * S, H)
        Wg = dequant_nvfp4(gate_W_packed, gate_scales)
        Wu = dequant_nvfp4(up_W_packed, up_scales)
        Wd = dequant_nvfp4(down_W_packed, down_scales)
        gate = jnp.einsum('th,nh->tn', xt, Wg)
        up = jnp.einsum('th,nh->tn', xt, Wu)
        gelu = jnp.tanh(0.7978845608028654 * (gate + 0.044715 * gate ** 3)) * gate * 0.5 + gate * 0.5
        inter = gelu * up
        out = jnp.einsum('tn,hn->th', inter, Wd)
        return out.reshape(B, S, H)
    x = x + _L0_attn_ref(_L0_cond_ref(x, 1, L0_cond_rms_weight, cond_2048, L0_cond_Wk, L0_cond_Wo, L0_cond_ln_gamma, L0_cond_ln_beta), L0_attn_Wq, L0_attn_Wk, L0_attn_Wv, L0_attn_Wo, L0_attn_lambda_init)
    x = x + _L0_ffn_ref(_L0_cond2_ref(cond_2048, x, L0_cond2_W_ih, L0_cond2_W_hh, L0_cond2_b_ih, L0_cond2_b_hh), L0_ffn_gate_W_packed, L0_ffn_gate_scales, L0_ffn_up_W_packed, L0_ffn_up_scales, L0_ffn_down_W_packed, L0_ffn_down_scales)
    return x

_drawn_inputs = setup_inputs


def setup_inputs(seed=0):
    import zlib

    import numpy as np

    out = dict(_drawn_inputs(seed))
    spreads = {'L0_cond_rms_weight': (1.0, 0.2),
     'L0_cond_ln_gamma': (1.0, 0.2),
     'L0_cond_ln_beta': (0.0, 0.1),
     'L0_attn_lambda_init': (-0.20000000298023224, 0.6),
     'L0_cond2_b_ih': (0.0, 0.1),
     'L0_cond2_b_hh': (0.0, 0.1)}
    factors = {}
    for name, (base, spread) in spreads.items():
        noise = np.random.default_rng([zlib.crc32(name.encode()), seed]).standard_normal(out[name].shape)
        drawn = base * np.exp(spread * noise) if base else spread * noise
        out[name] = jnp.asarray(drawn.astype(out[name].dtype))
    for name, factor in factors.items():
        out[name] = (out[name] * factor).astype(out[name].dtype)
    return out
```

```python
from contextlib import ExitStack

import numpy as np

import concourse.bass as bass
from concourse import mybir

F32 = mybir.dt.float32
BF16 = mybir.dt.bfloat16
I32 = mybir.dt.int32
ALU = mybir.AluOpType
ACT = mybir.ActivationFunctionType
AX = mybir.AxisListType.X

P = 128
B, T, D = 8, 128, 256
KT = D // P
NBLK = 8
BLK = T // NBLK
H = 16
HD = 128
HHD = HD // 2
SCALE = 1.0 / float(np.sqrt(HHD))
GB = 4
NG = B // GB
UNITS = NG * H
PAIRS = UNITS // 2
W4 = GB * T
MLP = 2048
MT = MLP // P
QB = 32
PK = 3 * P
NQ = 2 * PK // QB
GATES = 3 * D
STEPS = 16
CHUNKS = T // STEPS
HALF = STEPS // 2
TOK = STEPS * B
NJ = 4
MJ = MT // NJ
EPS_RMS = 1e-6
EPS_LN = 1e-6
MASKED = -1e30
GELU_A = 0.044715
GELU_C = 0.7978845608028654


def build(nc, x, cond, rms_weight, Wk_c, Wo_c, ln_gamma, ln_beta, Wq, Wk, Wv, Wo, lambda_init,
          W_ih, W_hh, b_ih, b_hh, gate_W, gate_s, up_W, up_s, down_W, down_s, out):
    ctx = ExitStack()
    with ctx:
        def sb(name, shape, dt=F32):
            return ctx.enter_context(nc.sbuf_tensor(name, shape, dt))

        def sem(name):
            return ctx.enter_context(nc.semaphore(name))

        bank = [ctx.enter_context(nc.psum_tensor(f"bank{i}", [P, 512], F32)) for i in range(8)]

        ident = sb("ident", [P, P])
        ident_h = sb("ident_h", [P, P], BF16)
        mask = sb("mask", [P, GB, T], BF16)
        block_of = sb("block_of", [P, NBLK])
        batch_of = sb("batch_of", [B, B, P])
        ones_row = sb("ones_row", [1, P])
        bias_pick = sb("bias_pick", [2, 3, HALF * B])

        x_sb = sb("x_sb", [P, B, D])
        xn = sb("xn", [P, B, D])
        wk_c = sb("wk_c", [P, KT, D])
        wo_c = sb("wo_c", [P, KT, D])
        wkT_c = sb("wkT_c", [P, KT, D])
        woT_c = sb("woT_c", [P, KT, D])
        gamma = sb("gamma", [P, KT])
        beta = sb("beta", [P, KT])
        rmsw_b = sb("rmsw_b", [B * NBLK, D])
        query_b = sb("query_b", [B * NBLK, D])
        wquery = sb("wquery", [B * NBLK, D])
        cond_sb = sb("cond_sb", [B, D])
        blocksT = sb("blocksT", [P, KT, B * NBLK])
        junk64 = sb("junk64", [B * NBLK, D])
        junk64a = sb("junk64a", [B * NBLK, D])
        dot = sb("dot", [B * NBLK, 1])
        ssq = sb("ssq", [B * NBLK, 1])
        ms = sb("ms", [B * NBLK, 1])
        rms = sb("rms", [B * NBLK, 1])
        rrms = sb("rrms", [B * NBLK, 1])
        score_c = sb("score_c", [B * NBLK, 1])
        row_max = sb("row_max", [1, B])
        row_s = sb("row_s", [1, B, NBLK])
        row_e = sb("row_e", [1, B, NBLK])
        row_sum = sb("row_sum", [1, B])
        row_r = sb("row_r", [1, B])
        row_p = sb("row_p", [1, B, NBLK])
        weighted = sb("weighted", [P, KT, B * NBLK])
        attendedT = sb("attendedT", [P, KT, B])
        proj = sb("proj", [B, D])
        stats = sb("stats", [P, B, 6])
        meanvar = sb("meanvar", [P, B, 2])
        var_e = sb("var_e", [P, B])
        std = sb("std", [P, B])
        rstd = sb("rstd", [P, B])
        xT = sb("xT", [P, KT, B, T])
        hT = sb("hT", [P, KT, B * T])
        lam = sb("lam", [P, H])
        lam_e = sb("lam_e", [P, H])
        lam_1 = sb("lam_1", [P, H])
        lam_r = sb("lam_r", [P, H])
        neg_lam = sb("neg_lam", [P, H])

        wqkv = [sb(f"wqkv{i}", [P, 3, KT, HD]) for i in range(2)]
        wo = [sb(f"wo{i}", [P, D]) for i in range(2)]
        qT = sb("qT", [P, W4])
        kT = sb("kT", [P, W4])
        v = [sb(f"v{i}", [P, GB, HD]) for i in range(2)]
        neg_max = sb("neg_max", [P, 2, GB])
        exps = sb("exps", [P, 2, GB, T])
        sums = sb("sums", [P, 2, GB])
        rsums = sb("rsums", [P, 2, GB])
        coef2 = sb("coef2", [P, GB])
        probs1 = sb("probs1", [P, GB, T])
        diff = sb("diff", [P, GB, T])
        diffT = sb("diffT", [P, W4])
        attT = sb("attT", [P, W4])
        x2T = sb("x2T", [P, KT, T, B])
        packed = sb("packed", [P, 3, P], I32)
        scales = sb("scales", [P, NQ])
        code = sb("code", [P, PK, 2], I32)
        sign = sb("sign", [P, PK, 2], I32)
        line2 = sb("line2", [P, PK, 2])
        line3 = sb("line3", [P, PK, 2])
        mag = sb("mag", [P, PK, 2])
        value = sb("value", [P, PK, 2])
        wscaled = sb("wscaled", [P, NQ, QB])
        wguT = sb("wguT", [P, 2 * KT, MLP])
        wdT = sb("wdT", [P, MT, D])

        wih = sb("wih", [P, KT, GATES])
        whh = sb("whh", [P, KT, GATES])
        biases = sb("biases", [2, GATES])
        ring = sb("ring", [P, KT, STEPS, B])
        hchunk = sb("hchunk", [P, KT, TOK])
        rz = sb("rz", [P, 2 * KT, B])
        n_g = sb("n_g", [P, KT, B])
        r_hn = sb("r_hn", [P, KT, B])
        n_pre = sb("n_pre", [P, KT, B])
        zc = sb("zc", [P, KT, B])
        zh = sb("zh", [P, KT, B])
        zn = sb("zn", [P, KT, B])
        g_sq = sb("g_sq", [P, 512])
        g_poly = sb("g_poly", [P, 512])
        g_arg = sb("g_arg", [P, 512])
        g_tanh = sb("g_tanh", [P, 512])
        g_lin = sb("g_lin", [P, 512])
        inter = [sb(f"inter{i}", [P, 512]) for i in range(2)]
        fin = sb("fin", [P, KT, B, STEPS])
        out_sb = sb("out_sb", [P, D])

        x_in = [sem(f"x_in{i}") for i in range(2)]
        wc_in, row_in, gru_in = sem("wc_in"), sem("row_in"), sem("gru_in")
        consts = sem("consts")
        pool_zero = sem("pool_zero")
        wcT_mm, wcT_ev_v, wcT_ev_a = sem("wcT_mm"), sem("wcT_ev_v"), sem("wcT_ev_a")
        blocks_mm, blocks_ev = sem("blocks_mm"), sem("blocks_ev")
        dot_done, h_ready = sem("dot_done"), sem("h_ready")
        xT_mm, xT_ev = sem("xT_mm"), sem("xT_ev")
        keys_mm, ssq_done, rms_done = sem("keys_mm"), sem("ssq_done"), sem("rms_done")
        ms_done, score_done, score_mm = sem("ms_done"), sem("score_done"), sem("score_mm")
        rows_done, rexp_done, probs_done = sem("rows_done"), sem("rexp_done"), sem("probs_done")
        bcast_mm, att_done, proj_mm, proj_ev = sem("bcast_mm"), sem("att_done"), sem("proj_mm"), sem("proj_ev")
        projb_mm, var_done, std_done, xn_done = sem("projb_mm"), sem("var_done"), sem("std_done"), sem("xn_done")
        hT_mm, hT_ev = sem("hT_mm"), sem("hT_ev")
        lam_exp, lam_done = sem("lam_exp"), sem("lam_done")
        dve1 = sem("dve1")
        wqkv_in = [sem(f"wqkv_in{i}") for i in range(2)]
        wo_in = [sem(f"wo_in{i}") for i in range(2)]
        packed_in = sem("packed_in")
        q_mm, k_mm, v_mm, s_mm = sem("q_mm"), sem("k_mm"), sem("v_mm"), sem("s_mm")
        t_mm, wo_mm, o_mm = sem("t_mm"), sem("wo_mm"), sem("o_mm")
        q_ev, k_ev, v_ev, t_ev, o_ev = sem("q_ev"), sem("k_ev"), sem("v_ev"), sem("t_ev"), sem("o_ev")
        max_done, exp_done = sem("max_done"), sem("exp_done")
        rsum_done, coef_done, diff_done = sem("rsum_done"), sem("coef_done"), sem("diff_done")
        bits_done, lines_done, mag_done = sem("bits_done"), sem("lines_done"), sem("mag_done")
        value_done, wscaled_done, deq_mm, deq_ev = sem("value_done"), sem("wscaled_done"), sem("deq_mm"), sem("deq_ev")
        y_ev = sem("y_ev")
        step_mm, rz_act, n_act = sem("step_mm"), sem("rz_act"), sem("n_act")
        rhn_done, npre_done, zc_done, zn_done = sem("rhn_done"), sem("npre_done"), sem("zc_done"), sem("zn_done")
        hchunk_done = sem("hchunk_done")
        gate_mm, up_mm, down_mm = sem("gate_mm"), sem("up_mm"), sem("down_mm")
        sq_done, poly_done, arg_done, tanh_done = sem("sq_done"), sem("poly_done"), sem("arg_done"), sem("tanh_done")
        lin_done, inter_done, fin_done = sem("lin_done"), sem("inter_done"), sem("fin_done")
        tr_mm, tr_ev, stored = sem("tr_mm"), sem("tr_ev"), sem("stored")

        def cols(b, n, k):
            return bank[b][:, 0:n * k].rearrange("p (n k) -> p n k", n=n)

        QB_, KB_, VB_, SB_, TO_, YB_ = 0, 1, 2, (3, 4), 5, (6, 7)
        GI_, GATE_, UP_, DOWN_, TR_ = (0, 1), (2, 3), (4, 5), 6, 7
        n_rows = 5

        block = ctx.enter_context(nc.Block())

        def attention(eng, step):
            for g in range(NG):
                first, last = g * H // 2, (g + 1) * H // 2 - 1
                for p in (first,):
                    for par in range(2):
                        step(p, 2 * p + par, par, g)
                with eng.Fori(first + 1, last) as p:
                    for par in range(2):
                        step(p, p * 2 + par, par, g)
                for par in range(2):
                    step(last, 2 * last + par, par, g)

        def chunks(eng, chunk):
            chunk(0, True, False, True)
            with eng.Fori(1, CHUNKS - 1) as c:
                chunk(c, True, True, True)
            chunk(CHUNKS - 1, True, True, False)
            chunk(CHUNKS, False, True, False)

        @block.sync
        def _(sp):
            x_src = x.rearrange("b t d -> t b d")
            for i in range(2):
                sp.dma_start(x_sb[:, i * GB:(i + 1) * GB, :], x_src[:, i * GB:(i + 1) * GB, :]).then_inc(x_in[i], 16)

            def load_wqkv(u, par, h):
                if not (isinstance(u, int) and u < 2):
                    sp.wait_ge(v_mm, u - 1)
                for i, w in enumerate((Wq, Wk, Wv)):
                    src = w.rearrange("(k p) n -> p k n", p=P)
                    sp.dma_start(wqkv[par][:, i, :, :], src[:, :, bass.ds(h * HD, HD)]).then_inc(wqkv_in[par], 16)

            def load_wo(u, par, h):
                if not (isinstance(u, int) and u < 2):
                    sp.wait_ge(wo_mm, u - 1)
                sp.dma_start(wo[par][:, :], Wo[bass.ds(h * HD, HD), :]).then_inc(wo_in[par], 16)

            def load_packed(p):
                if not (isinstance(p, int) and p < 1):
                    sp.wait_ge(wscaled_done, p)
                sp.dma_start(packed[:, 0, :], gate_W[bass.ds(p * P, P), :]).then_inc(packed_in, 16)
                sp.dma_start(packed[:, 1, :], up_W[bass.ds(p * P, P), :]).then_inc(packed_in, 16)
                sp.dma_start(packed[:, 2, :].rearrange("p (k m) -> p k m", k=KT),
                             down_W.rearrange("(k p) m -> p k m", p=P)[:, :, bass.ds(p * (P // 2), P // 2)]).then_inc(packed_in, 16)
                sp.dma_start(scales[:, 0:8], gate_s[bass.ds(p * P, P), :]).then_inc(packed_in, 16)
                sp.dma_start(scales[:, 8:16], up_s[bass.ds(p * P, P), :]).then_inc(packed_in, 16)
                sp.dma_start(scales[:, 16:24].rearrange("p (k m) -> p k m", k=KT),
                             down_s.rearrange("(k p) m -> p k m", p=P)[:, :, bass.ds(p * 4, 4)]).then_inc(packed_in, 16)

            load_wqkv(0, 0, 0)
            load_packed(0)
            sp.dma_start(wih[:, :, :], W_ih.rearrange("(k p) n -> p k n", p=P)).then_inc(gru_in, 16)
            sp.dma_start(whh[:, :, :], W_hh.rearrange("(k p) n -> p k n", p=P)).then_inc(gru_in, 16)
            sp.dma_start(biases[0:1, :], b_ih.rearrange("(a n) -> a n", a=1)).then_inc(gru_in, 16)
            sp.dma_start(biases[1:2, :], b_hh.rearrange("(a n) -> a n", a=1)).then_inc(gru_in, 16)

            def step(p, u, par, g):
                h = u - g * H
                if isinstance(u, int) and h == H - 1:
                    if g < NG - 1:
                        load_wqkv(u + 1, 1 - par, 0)
                else:
                    load_wqkv(u + 1, 1 - par, h + 1)
                load_wo(u, par, h)
                if par == 1 and not (isinstance(p, int) and p == PAIRS - 1):
                    load_packed(p + 1)

            attention(sp, step)

            def store(c, gru, mlp, more):
                if not mlp:
                    return
                sp.wait_ge(tr_ev, c)
                sp.dma_start(out[:, bass.ds((c - 1) * STEPS, STEPS), :],
                             out_sb[:, :]).then_inc(stored, 16)

            chunks(sp, store)
            sp.wait_ge(stored, 16 * CHUNKS)

        @block.gpsimd
        def _(pool):
            pool.memset(ident[:, :], 0.0).then_inc(pool_zero, 1)
            pool.memset(mask[:, :, :], 0.0).then_inc(pool_zero, 1)
            pool.memset(block_of[:, :], 1.0).then_inc(pool_zero, 1)
            pool.memset(batch_of[:, :, :], 0.0).then_inc(pool_zero, 1)
            pool.memset(bias_pick[:, :, :], 1.0).then_inc(pool_zero, 1)
            pool.memset(ones_row[:, :], 1.0).then_inc(consts, 1)
            pool.wait_ge(pool_zero, 5)
            pool.affine_select(out=ident[:, :], in_=ident[:, :], compare_op=ALU.not_equal, fill=1.0, base=0,
                               pattern=[[-1, P]], channel_multiplier=1).then_inc(pool_zero, 1)
            pool.affine_select(out=mask[:, :, :], in_=mask[:, :, :], compare_op=ALU.is_ge, fill=MASKED, base=0,
                               pattern=[[0, GB], [-1, T]], channel_multiplier=1).then_inc(consts, 1)
            pool.affine_select(out=block_of[:, :], in_=block_of[:, :], compare_op=ALU.is_ge, fill=0.0, base=0,
                               pattern=[[-BLK, NBLK]], channel_multiplier=1).then_inc(pool_zero, 1)
            pool.affine_select(out=batch_of[:, :, :], in_=batch_of[:, :, :], compare_op=ALU.not_equal, fill=1.0,
                               base=0, pattern=[[-1, B], [0, P]], channel_multiplier=1).then_inc(consts, 1)
            pool.affine_select(out=bias_pick[:, 1, :], in_=bias_pick[:, 1, :], compare_op=ALU.is_ge, fill=0.0,
                               base=0, pattern=[[0, HALF * B]], channel_multiplier=-1).then_inc(consts, 1)
            pool.affine_select(out=bias_pick[:, 2, :], in_=bias_pick[:, 2, :], compare_op=ALU.is_ge, fill=0.0,
                               base=-1, pattern=[[0, HALF * B]], channel_multiplier=1).then_inc(consts, 1)
            pool.wait_ge(pool_zero, 7)
            pool.tensor_copy(ident_h[:, :], ident[:, :]).then_inc(consts, 1)
            pool.affine_select(out=block_of[:, :], in_=block_of[:, :], compare_op=ALU.is_ge, fill=0.0,
                               base=BLK - 1, pattern=[[BLK, NBLK]], channel_multiplier=-1).then_inc(consts, 1)

        NCONST = 8

        @block.tensor
        def _(pe):
            pe.wait_ge(consts, NCONST - 1)
            pe.wait_ge(wc_in, 32)
            for i, (w, b) in enumerate(((wk_c, 0), (wo_c, 1))):
                dst = cols(b, KT, D)
                for c in range(KT):
                    for r in range(KT):
                        last = pe.transpose(dst[:, c, r * P:(r + 1) * P], w[:, r, c * P:(c + 1) * P], ident[:, :])
                last.then_inc(wcT_mm, 1)
            blk = bank[2][:, 0:KT * B * NBLK].rearrange("p (k b n) -> p k b n", k=KT, b=B)
            for b in range(B):
                if b % GB == 0:
                    pe.wait_ge(x_in[b // GB], 16)
                for k in range(KT):
                    last = pe.matmul(blk[:, k, b, :], x_sb[:, b, k * P:(k + 1) * P], block_of[:, :],
                                     start=True, stop=True)
            pe.wait_ge(row_in, 16 * n_rows)
            h0 = bank[2][:, 256:256 + KT * B].rearrange("p (k b) -> p k b", k=KT)
            for k in range(KT):
                last = pe.transpose(h0[:, k, :], cond_sb[:, k * P:(k + 1) * P], ident[0:B, 0:B])
            last.then_inc(blocks_mm, 1)
            pe.wait_ge(blocks_ev, 1)
            pe.wait_ge(wcT_ev_v, 1)
            for k in range(KT):
                last = pe.matmul(bank[3][0:B * NBLK, 0:D], blocksT[:, k, :], wkT_c[:, k, :],
                                 start=(k == 0), stop=(k == KT - 1))
            last.then_inc(keys_mm, 1)
            for b in range(B):
                for k in range(KT):
                    n = (k * B + b)
                    last = pe.transpose(bank[4 + n // 4][:, n % 4 * T:(n % 4 + 1) * T],
                                        x_sb[:, b, k * P:(k + 1) * P], ident[:, :])
            last.then_inc(xT_mm, 1)
            pe.wait_ge(score_done, 1)
            pe.transpose(bank[3][0:1, 256:256 + B * NBLK], score_c[:, :], ident[0:B * NBLK, 0:B * NBLK]).then_inc(score_mm, 1)
            pe.wait_ge(probs_done, 1)
            pe.matmul(bank[0][:, 0:B * NBLK], ones_row[:, :], row_p.rearrange("a b n -> a (b n)"),
                      start=True, stop=True).then_inc(bcast_mm, 1)
            pe.wait_ge(att_done, 1)
            pe.wait_ge(wcT_ev_a, 1)
            for k in range(KT):
                last = pe.matmul(bank[1][0:B, 0:D], attendedT[:, k, :], woT_c[:, k, :],
                                 start=(k == 0), stop=(k == KT - 1))
            last.then_inc(proj_mm, 1)
            pe.wait_ge(proj_ev, 1)
            pe.wait_ge(xT_ev, 4)
            for b in range(B):
                last = pe.matmul(cols(4 + b // 2, 2, D)[:, b % 2, :], batch_of[:, b, :], proj[:, :],
                                 start=True, stop=True)
                if b % 2:
                    last.then_inc(projb_mm, 1)
            for b in range(B):
                pe.wait_ge(xn_done, b + 1)
                for k in range(KT):
                    last = pe.transpose(bank[NG * k + b // GB][:, b % GB * T:(b % GB + 1) * T],
                                        xn[:, b, k * P:(k + 1) * P], ident[:, :])
                if b % GB == GB - 1:
                    last.then_inc(hT_mm, 1)
            pe.wait_ge(hT_ev, 4)
            pe.wait_ge(lam_done, 1)

            def project(p, u, par, g):
                w = wqkv[par]
                pe.wait_ge(wqkv_in[par], p * 48 + 48)
                for i, (b, done) in enumerate(((QB_, q_mm), (KB_, k_mm))):
                    for k in range(KT):
                        last = pe.matmul(bank[b][:, :], w[:, i, k, :], hT[:, k, g * W4:(g + 1) * W4],
                                         start=(k == 0), stop=(k == KT - 1))
                    last.then_inc(done, 1)
                if not (isinstance(u, int) and u == 0):
                    pe.wait_ge(v_ev, u)
                if not (isinstance(u, int) and u <= 2):
                    pe.wait_ge(deq_ev, 2 * (p - 1 + par))
                for b in range(GB):
                    for k in range(KT):
                        t0 = (g * GB + b) * T
                        last = pe.matmul(bank[VB_][:, b * HD:(b + 1) * HD], hT[:, k, t0:t0 + T], w[:, 2, k, :],
                                         start=(k == 0), stop=(k == KT - 1))
                last.then_inc(v_mm, 1)

            def turn_weights(p):
                pe.wait_ge(wscaled_done, p + 1)
                src = wscaled.rearrange("p n q -> p (n q)")
                for n in range(4):
                    last = pe.transpose(bank[TO_][:, n * P:(n + 1) * P], src[:, n * P:(n + 1) * P], ident[:, :])
                last.then_inc(deq_mm, 1)
                for n in range(2):
                    last = pe.transpose(bank[VB_][:, n * P:(n + 1) * P], src[:, (4 + n) * P:(5 + n) * P], ident[:, :])
                last.then_inc(deq_mm, 1)

            def project_out(u, par, start, stop):
                pe.wait_ge(wo_in[par], (u - par) * 8 + 16)
                pe.wait_ge(o_ev, u + 1)
                for f in range(KT):
                    last = pe.matmul(bank[YB_[f]][:, :], wo[par][:, f * P:(f + 1) * P], attT[:, :],
                                     start=start, stop=stop, skip_group_check=True)
                last.then_inc(wo_mm, 1)

            def step(p, u, par, g):
                at = u - g * H if isinstance(u, int) else -1
                if not (isinstance(u, int) and u == 0):
                    pe.wait_ge(o_ev, u)
                if par == 0 and not (isinstance(p, int) and p == 0):
                    pe.wait_ge(v_ev, u + 1)
                    turn_weights(p - 1)
                pe.wait_ge(q_ev, u + 1)
                pe.wait_ge(k_ev, u + 1)
                if not (isinstance(u, int) and u == 0):
                    pe.wait_ge(exp_done, u)
                for i in range(2):
                    pe.matmul(bank[SB_[i]][:, :], ident_h[:, :], mask.rearrange("p b s -> p (b s)"),
                              start=True, stop=False, skip_group_check=True)
                for b in range(GB):
                    for i in range(2):
                        rows = slice(i * HHD, (i + 1) * HHD)
                        last = pe.matmul(bank[SB_[i]][:, b * T:(b + 1) * T], qT[rows, b * T:(b + 1) * T],
                                         kT[rows, b * T:(b + 1) * T], start=False, stop=(b == GB - 1),
                                         skip_group_check=True)
                last.then_inc(s_mm, 1)
                if not (isinstance(u, int) and u == UNITS - 1):
                    project(p + par, u + 1, 1 - par, g + (at == H - 1))
                pe.wait_ge(diff_done, u + 1)
                if not (isinstance(p, int) and p == 0):
                    pe.wait_ge(deq_ev, 2 * p)
                for b in range(GB):
                    last = pe.transpose(bank[TO_][:, b * T:(b + 1) * T], diff[:, b, :], ident[:, :])
                last.then_inc(t_mm, 1)
                if not (isinstance(u, int) and u == 0):
                    if at == 1 and g > 0:
                        pe.wait_ge(y_ev, g)
                    project_out(u - 1, 1 - par, start=(at == 1), stop=(at == 0))
                pe.wait_ge(t_ev, u + 1)
                pe.wait_ge(v_ev, u + 1)
                for b in range(GB):
                    last = pe.matmul(bank[TO_][:, b * T:(b + 1) * T], v[par][:, b, :], diffT[:, b * T:(b + 1) * T],
                                     start=True, stop=True)
                last.then_inc(o_mm, 1)

            project(0, 0, 0, 0)
            attention(pe, step)
            project_out(UNITS - 1, 1, start=False, stop=True)
            turn_weights(PAIRS - 1)

            pe.wait_ge(gru_in, 80)
            pe.wait_ge(y_ev, NG)
            pe.wait_ge(deq_ev, 2 * PAIRS)

            def gates_in(half, t0):
                gi = bank[GI_[half]][:, :].rearrange("p (g c) -> p g c", g=8)
                for n, (gate, pick) in enumerate([(0, 0), (1, 0), (2, 0), (3, 0), (4, 2), (5, 2), (4, 1), (5, 1)]):
                    own = pick == 2
                    last = pe.matmul(gi[:, n, :], biases[:, gate * P:(gate + 1) * P], bias_pick[:, pick, :],
                                     start=(n == 0), stop=False, skip_group_check=True)
                    if own:
                        continue
                    for k in range(KT):
                        rhs = x2T[:, k, bass.ds(t0, HALF), :]
                        last = pe.matmul(gi[:, n, :], wih[:, k, gate * P:(gate + 1) * P],
                                         rhs, start=False, stop=(k == KT - 1),
                                         skip_group_check=True)

            def recur(s):
                gi = bank[GI_[s // HALF]][:, :].rearrange("p (g t b) -> p g t b", g=8, t=HALF)
                for gate in range(GATES // P):
                    for k in range(KT):
                        last = pe.matmul(gi[:, gate, s % HALF, :], whh[:, k, gate * P:(gate + 1) * P],
                                         ring[:, k, (s - 1) % STEPS, :], start=False, stop=(k == KT - 1),
                                         skip_group_check=True)
                last.then_inc(step_mm, 1)

            def hidden(f, j, up):
                if j == 0 and not up:
                    pe.wait_ge(hchunk_done, f + 1)
                if not up and not (isinstance(f, int) and f == 0 and j < 2):
                    pe.wait_ge(inter_done, f * MJ + max(j - 1, 0))
                dst = bank[(UP_ if up else GATE_)[j % 2]]
                for n in range(NJ):
                    m = NJ * j + n
                    for k in range(KT):
                        last = pe.matmul(dst[:, n * TOK:(n + 1) * TOK], wguT[:, (KT if up else 0) + k, m * P:(m + 1) * P],
                                         hchunk[:, k, :], start=(k == 0), stop=(k == KT - 1))
                last.then_inc(up_mm if up else gate_mm, 1)

            def down(f, j):
                pe.wait_ge(inter_done, f * MJ + (j + 1))
                if j == 0 and not (isinstance(f, int) and f == 0):
                    pe.wait_ge(fin_done, f)
                for n in range(NJ):
                    m = NJ * j + n
                    for o in range(KT):
                        last = pe.matmul(bank[DOWN_][:, o * TOK:(o + 1) * TOK], wdT[:, m, o * P:(o + 1) * P],
                                         inter[j % 2][:, n * TOK:(n + 1) * TOK], start=(m == 0 and o == 0),
                                         stop=(m == MT - 1), skip_group_check=True)
                last.then_inc(down_mm, 1)

            def turn_out(f):
                pe.wait_ge(fin_done, f + 1)
                if not (isinstance(f, int) and f == 0):
                    pe.wait_ge(tr_ev, f)
                for o in range(KT):
                    last = pe.transpose(bank[TR_][:, o * P:(o + 1) * P],
                                        fin[:, o, :, :].rearrange("p b t -> p (b t)"), ident[:, :])
                last.then_inc(tr_mm, 1)

            def chunk(c, gru, mlp, more):
                f = c - 1
                for s in range(STEPS):
                    if gru:
                        pe.wait_ge(h_ready, c * STEPS + (s + 1))
                        recur(s)
                        if s == 2:
                            gates_in(1, c * STEPS + HALF)
                        if s == 12 and more:
                            gates_in(0, c * STEPS + STEPS)
                    if mlp:
                        if s % 3 == 0 and s // 3 < MJ:
                            hidden(f, s // 3, False)
                        if s % 3 == 1 and s // 3 < MJ:
                            hidden(f, s // 3, True)
                        if s >= 5 and (s - 5) % 3 == 0:
                            down(f, (s - 5) // 3)
                if mlp:
                    turn_out(f)

            gates_in(0, 0)
            chunks(pe, chunk)

        @block.scalar
        def _(act):
            act.dma_start(wk_c[:, :, :], Wk_c.rearrange("(k p) n -> p k n", p=P)).then_inc(wc_in, 16)
            act.dma_start(wo_c[:, :, :], Wo_c.rearrange("(k p) n -> p k n", p=P)).then_inc(wc_in, 16)
            act.dma_start(rmsw_b[:, :], rms_weight.rearrange("(a n) -> a n", a=1).broadcast_to([B * NBLK, D])).then_inc(row_in, 16)
            act.dma_start(query_b[:, :], cond[1:2, :].broadcast_to([B * NBLK, D])).then_inc(row_in, 16)
            act.dma_start(cond_sb[:, :], cond).then_inc(row_in, 16)
            act.dma_start(lam[:, :], lambda_init.rearrange("(a n) -> a n", a=1).broadcast_to([P, H])).then_inc(row_in, 16)
            with nc.allow_non_contiguous_dma(reason="two short vectors onto partitions"):
                act.dma_start(gamma[:, :], ln_gamma.rearrange("(k p) -> p k", p=P)).then_inc(row_in, 8 * 2)
                act.dma_start(beta[:, :], ln_beta.rearrange("(k p) -> p k", p=P)).then_inc(gru_in, 16)

            act.wait_ge(row_in, 16 * n_rows)
            act.activation(lam_e[:, :], lam[:, :], ACT.Exp, scale=-1.0).then_inc(lam_exp, 1)
            act.wait_ge(wcT_mm, 2)
            act.activation(woT_c[:, :, :], cols(1, KT, D), ACT.Copy).then_inc(wcT_ev_a, 1)
            act.wait_ge(dot_done, 1)
            act.activation(junk64a[:, :], bank[3][0:B * NBLK, 0:D], ACT.Square, accum_out=ssq[:, :]).then_inc(ssq_done, 1)
            act.wait_ge(xT_mm, 1)
            xT_flat = xT.rearrange("p k b t -> p (k b t)")
            for n in range(2):
                act.activation(xT_flat[:, n * 512:(n + 1) * 512], bank[4 + n][:, :], ACT.Copy).then_inc(xT_ev, 1)
            act.wait_ge(ms_done, 1)
            act.activation(rms[:, :], ms[:, :], ACT.Sqrt).then_inc(rms_done, 1)
            for n in range(2, 4):
                act.activation(xT_flat[:, n * 512:(n + 1) * 512], bank[4 + n][:, :], ACT.Copy).then_inc(xT_ev, 1)
            act.wait_ge(rows_done, 1)
            act.activation(row_e[:, :, :], row_s[:, :, :], ACT.Exp).then_inc(rexp_done, 1)
            act.wait_ge(var_done, 1)
            act.activation(std[:, :], var_e[:, :], ACT.Sqrt).then_inc(std_done, 1)
            act.wait_ge(gru_in, 80)
            for g in range(NG):
                act.wait_ge(hT_mm, g + 1)
                for k in range(KT):
                    act.activation(hT[:, k, g * W4:(g + 1) * W4], bank[NG * k + g][:, :], ACT.Identity,
                                   bias=beta[:, k:k + 1], scale=gamma[:, k:k + 1]).then_inc(hT_ev, 1)

            def keys_values(u, par):
                act.wait_ge(k_mm, u + 1)
                act.activation(kT[:, :], bank[KB_][:, :], ACT.Copy).then_inc(k_ev, 1)
                act.wait_ge(v_mm, u + 1)
                act.activation(v[par][:, :, :], cols(VB_, GB, HD), ACT.Copy).then_inc(v_ev, 1)

            def keep_weights(p):
                act.wait_ge(deq_mm, 2 * p + 1)
                act.activation(wguT[:, :, bass.ds(p * P, P)], cols(TO_, 2 * KT, P), ACT.Copy).then_inc(deq_ev, 1)
                act.wait_ge(deq_mm, 2 * p + 2)
                act.activation(wdT[:, bass.ds(p, 1), :].rearrange("p a d -> p (a d)"), bank[VB_][:, 0:D], ACT.Copy).then_inc(deq_ev, 1)

            def step(p, u, par, g):
                if par == 0 and not (isinstance(p, int) and p == 0):
                    keep_weights(p - 1)
                if not (isinstance(u, int) and u == 0):
                    act.wait_ge(diff_done, u)
                for i in range(2):
                    act.wait_ge(max_done, 2 * u + (i + 1))
                    for b in range(GB):
                        last = act.activation(exps[:, i, b, :], bank[SB_[i]][:, b * T:(b + 1) * T], ACT.Exp,
                                              bias=neg_max[:, i, b:b + 1], scale=1.0,
                                              accum_out=sums[:, i, b:b + 1])
                last.then_inc(exp_done, 1)
                if not (isinstance(u, int) and u == UNITS - 1):
                    keys_values(u + 1, 1 - par)
                act.wait_ge(t_mm, u + 1)
                act.activation(diffT[:, :], bank[TO_][:, :], ACT.Copy).then_inc(t_ev, 1)

            keys_values(0, 0)
            attention(act, step)
            keep_weights(PAIRS - 1)

            def chunk(c, gru, mlp, more):
                f = c - 1
                for s in range(STEPS):
                    if gru:
                        t = c * STEPS + s
                        gi = bank[GI_[s // HALF]][:, :].rearrange("p (g t b) -> p g t b", g=8, t=HALF)
                        act.wait_ge(step_mm, t + 1)
                        act.activation(rz[:, :, :], gi[:, 0:4, s % HALF, :], ACT.Sigmoid).then_inc(rz_act, 1)
                        act.wait_ge(npre_done, t + 1)
                        act.activation(n_g[:, :, :], n_pre[:, :, :], ACT.Tanh).then_inc(n_act, 1)
                    if mlp:
                        if s % 3 == 1 and s // 3 < MJ:
                            j = s // 3
                            act.wait_ge(gate_mm, f * MJ + (j + 1))
                            if not (isinstance(f, int) and f == 0 and j == 0):
                                act.wait_ge(poly_done, f * MJ + j)
                            act.activation(g_sq[:, :], bank[GATE_[j % 2]][:, :], ACT.Square).then_inc(sq_done, 1)
                        if s % 3 == 0 and 3 <= s < 3 + 3 * MJ:
                            j = s // 3 - 1
                            act.wait_ge(arg_done, f * MJ + (j + 1))
                            if not (isinstance(f, int) and f == 0 and j == 0):
                                act.wait_ge(lin_done, f * MJ + j)
                            act.activation(g_tanh[:, :], g_arg[:, :], ACT.Tanh, scale=GELU_C).then_inc(tanh_done, 1)
                if mlp:
                    act.wait_ge(tr_mm, f + 1)
                    if not (isinstance(f, int) and f == 0):
                        act.wait_ge(stored, 16 * f)
                    act.activation(out_sb[:, :], bank[TR_][:, 0:D], ACT.Copy).then_inc(tr_ev, 1)

            chunks(act, chunk)

        @block.vector
        def _(dve):
            mark = [0]

            def then(ins):
                mark[0] += 1
                ins.then_inc(dve1, 1)
                dve.wait_ge(dve1, mark[0])

            dve.wait_ge(row_in, 16 * n_rows)
            then(dve.tensor_tensor(wquery[:, :], rmsw_b[:, :], query_b[:, :], ALU.mult))
            dve.wait_ge(wcT_mm, 1)
            dve.tensor_copy(wkT_c[:, :, :], cols(0, KT, D)).then_inc(wcT_ev_v, 1)
            dve.wait_ge(blocks_mm, 1)
            dve.tensor_copy(blocksT[:, :, :], cols(2, KT, B * NBLK)).then_inc(blocks_ev, 1)
            dve.tensor_copy(ring[:, :, STEPS - 1, :],
                            bank[2][:, 256:256 + KT * B].rearrange("p (k b) -> p k b", k=KT)).then_inc(h_ready, 1)
            dve.wait_ge(lam_exp, 1)
            then(dve.tensor_scalar(lam_1[:, :], lam_e[:, :], 1.0, None, ALU.add))
            then(dve.reciprocal(lam_r[:, :], lam_1[:, :]))
            dve.tensor_scalar(neg_lam[:, :], lam_r[:, :], -1.0, None, ALU.mult).then_inc(lam_done, 1)
            dve.wait_ge(keys_mm, 1)
            dve.scalar_tensor_tensor(out=junk64[:, :], in0=bank[3][0:B * NBLK, 0:D], scalar=1.0, in1=wquery[:, :],
                                     op0=ALU.mult, op1=ALU.mult, accum_out=dot[:, :]).then_inc(dot_done, 1)
            dve.wait_ge(ssq_done, 1)
            dve.tensor_scalar(ms[:, :], ssq[:, :], 1.0 / D, EPS_RMS, ALU.mult, ALU.add).then_inc(ms_done, 1)
            dve.wait_ge(rms_done, 1)
            then(dve.reciprocal(rrms[:, :], rms[:, :]))
            dve.tensor_tensor(score_c[:, :], dot[:, :], rrms[:, :], ALU.mult).then_inc(score_done, 1)
            dve.wait_ge(score_mm, 1)
            row = bank[3][0:1, 256:256 + B * NBLK].rearrange("p (b n) -> p b n", b=B)
            then(dve.tensor_reduce(row_max[:, :], row, AX, ALU.max))
            dve.tensor_tensor(row_s[:, :, :], row, row_max[:, :].unsqueeze(2).broadcast_to([1, B, NBLK]),
                              ALU.subtract).then_inc(rows_done, 1)
            dve.wait_ge(rexp_done, 1)
            then(dve.tensor_reduce(row_sum[:, :], row_e[:, :, :], AX, ALU.add))
            then(dve.reciprocal(row_r[:, :], row_sum[:, :]))
            dve.tensor_tensor(row_p[:, :, :], row_e[:, :, :], row_r[:, :].unsqueeze(2).broadcast_to([1, B, NBLK]),
                              ALU.mult).then_inc(probs_done, 1)
            dve.wait_ge(bcast_mm, 1)
            then(dve.tensor_tensor(weighted[:, :, :], blocksT[:, :, :],
                                   bank[0][:, 0:B * NBLK].unsqueeze(1).broadcast_to([P, KT, B * NBLK]), ALU.mult))
            dve.tensor_reduce(attendedT[:, :, :], weighted.rearrange("p k (b n) -> p k b n", b=B), AX,
                              ALU.add).then_inc(att_done, 1)
            dve.wait_ge(proj_mm, 1)
            dve.tensor_copy(proj[:, :], bank[1][0:B, 0:D]).then_inc(proj_ev, 1)
            for i in range(B // 2):
                dve.wait_ge(projb_mm, i + 1)
                last = dve.tensor_tensor(xn[:, 2 * i:2 * i + 2, :], x_sb[:, 2 * i:2 * i + 2, :], cols(4 + i, 2, D), ALU.add)
            then(last)
            for b in range(B):
                last = dve.bn_stats(stats[:, b, :], xn[:, b, :])
            then(last)
            for b in range(B):
                last = dve.bn_aggr(meanvar[:, b, :], stats[:, b, :])
            then(last)
            dve.tensor_scalar(var_e[:, :], meanvar[:, :, 1], EPS_LN, None, ALU.add).then_inc(var_done, 1)
            dve.wait_ge(std_done, 1)
            then(dve.reciprocal(rstd[:, :], std[:, :]))
            for b in range(B):
                dve.tensor_scalar(xn[:, b, :], xn[:, b, :], meanvar[:, b, 0:1], rstd[:, b:b + 1], ALU.subtract,
                                  ALU.mult).then_inc(xn_done, 1)

            def queries(u):
                dve.wait_ge(q_mm, u + 1)
                dve.tensor_scalar(qT[:, :], bank[QB_][:, :], SCALE, None, ALU.mult).then_inc(q_ev, 1)

            def codes(p):
                dve.wait_ge(packed_in, p * 96 + 96)
                src = packed.rearrange("p a n -> p (a n)")
                dve.tensor_scalar(code[:, :, 0], src, 7, None, ALU.bitwise_and).then_inc(bits_done, 1)
                dve.tensor_scalar(code[:, :, 1], src, 4, 7, ALU.logical_shift_right, ALU.bitwise_and).then_inc(bits_done, 1)
                dve.tensor_scalar(sign[:, :, 0], src, 8, 28, ALU.bitwise_and, ALU.logical_shift_left).then_inc(bits_done, 1)
                dve.tensor_scalar(sign[:, :, 1], src, 128, 24, ALU.bitwise_and, ALU.logical_shift_left).then_inc(bits_done, 1)

            def magnitudes(p):
                dve.wait_ge(bits_done, 4 * p + 4)
                dve.tensor_scalar(line2[:, :, :], code[:, :, :], 1.0, -2.0, ALU.mult, ALU.add).then_inc(lines_done, 1)
                dve.tensor_scalar(line3[:, :, :], code[:, :, :], 2.0, -8.0, ALU.mult, ALU.add).then_inc(lines_done, 1)
                dve.wait_ge(lines_done, 2 * p + 2)
                dve.scalar_tensor_tensor(out=mag[:, :, :], in0=code[:, :, :], scalar=0.5, in1=line2[:, :, :],
                                         op0=ALU.mult, op1=ALU.max).then_inc(mag_done, 1)
                dve.wait_ge(mag_done, 2 * p + 1)
                dve.tensor_tensor(mag[:, :, :], mag[:, :, :], line3[:, :, :], ALU.max).then_inc(mag_done, 1)

            def weights(p):
                dve.wait_ge(mag_done, 2 * p + 2)
                dve.tensor_tensor(value[:, :, :].bitcast(I32), mag[:, :, :].bitcast(I32), sign[:, :, :],
                                  ALU.bitwise_or).then_inc(value_done, 1)
                dve.wait_ge(value_done, p + 1)
                if not (isinstance(p, int) and p == 0):
                    dve.wait_ge(deq_mm, 2 * p)
                dve.tensor_tensor(wscaled[:, :, :], value.rearrange("p (n q) i -> p n (q i)", n=NQ),
                                  scales[:, :].unsqueeze(2).broadcast_to([P, NQ, QB]), ALU.mult).then_inc(wscaled_done, 1)

            def step(p, u, par, g):
                h = u - g * H
                dve.wait_ge(s_mm, u + 1)
                if not (isinstance(u, int) and u == 0):
                    dve.wait_ge(exp_done, u)
                for i in range(2):
                    dve.tensor_reduce(neg_max[:, i, :], cols(SB_[i], GB, T), AX, ALU.max, negate=True).then_inc(max_done, 1)
                if par == 0:
                    codes(p)
                else:
                    weights(p)
                dve.wait_ge(exp_done, u + 1)
                dve.reciprocal(rsums[:, :, :], sums[:, :, :]).then_inc(rsum_done, 1)
                dve.wait_ge(rsum_done, u + 1)
                dve.tensor_scalar(coef2[:, :], rsums[:, 1, :], neg_lam[:, bass.ds(h, 1)], None, ALU.mult).then_inc(coef_done, 1)
                for b in range(GB):
                    last = dve.tensor_scalar(probs1[:, b, :], exps[:, 0, b, :], rsums[:, 0, b:b + 1], None, ALU.mult)
                last.then_inc(coef_done, 1)
                dve.wait_ge(coef_done, 2 * u + 2)
                for b in range(GB):
                    last = dve.scalar_tensor_tensor(out=diff[:, b, :], in0=exps[:, 1, b, :], scalar=coef2[:, b:b + 1],
                                                    in1=probs1[:, b, :], op0=ALU.mult, op1=ALU.add)
                last.then_inc(diff_done, 1)
                if not (isinstance(u, int) and u == UNITS - 1):
                    queries(u + 1)
                if par == 0:
                    magnitudes(p)
                dve.wait_ge(o_mm, u + 1)
                dve.tensor_copy(attT[:, :], bank[TO_][:, :]).then_inc(o_ev, 1)
                if isinstance(u, int) and u == H:
                    residual(0)

            def residual(g):
                dve.wait_ge(wo_mm, (g + 1) * H)
                for k in range(KT):
                    last = dve.tensor_tensor(x2T[:, k, :, g * GB:(g + 1) * GB].rearrange("p t b -> p b t"),
                                             cols(YB_[k], GB, T), xT[:, k, g * GB:(g + 1) * GB, :], ALU.add)
                last.then_inc(y_ev, 1)

            queries(0)
            attention(dve, step)
            residual(1)

            def chunk(c, gru, mlp, more):
                f = c - 1
                if mlp:
                    dve.wait_ge(h_ready, c * STEPS + 1)
                    if not (isinstance(f, int) and f == 0):
                        dve.wait_ge(up_mm, f * MJ)
                    dve.tensor_copy(hchunk[:, :, :], ring.rearrange("p k t b -> p k (t b)")).then_inc(hchunk_done, 1)
                for s in range(STEPS):
                    if gru:
                        t = c * STEPS + s
                        gi = bank[GI_[s // HALF]][:, :].rearrange("p (g t b) -> p g t b", g=8, t=HALF)
                        dve.wait_ge(rz_act, t + 1)
                        dve.tensor_tensor(r_hn[:, :, :], gi[:, 4:6, s % HALF, :], rz[:, 0:KT, :], ALU.mult).then_inc(rhn_done, 1)
                        dve.wait_ge(rhn_done, t + 1)
                        dve.tensor_tensor(n_pre[:, :, :], gi[:, 6:8, s % HALF, :], r_hn[:, :, :], ALU.add).then_inc(npre_done, 1)
                        dve.tensor_scalar(zc[:, :, :], rz[:, KT:, :], -1.0, 1.0, ALU.mult, ALU.add).then_inc(zc_done, 1)
                        dve.tensor_tensor(zh[:, :, :], rz[:, KT:, :], ring[:, :, (s - 1) % STEPS, :], ALU.mult)
                        dve.wait_ge(zc_done, t + 1)
                        dve.wait_ge(n_act, t + 1)
                        dve.tensor_tensor(zn[:, :, :], zc[:, :, :], n_g[:, :, :], ALU.mult).then_inc(zn_done, 1)
                        dve.wait_ge(zn_done, t + 1)
                        dve.tensor_tensor(ring[:, :, s, :], zn[:, :, :], zh[:, :, :], ALU.add).then_inc(h_ready, 1)
                    if mlp:
                        if s % 3 == 2 and s // 3 < MJ:
                            j = s // 3
                            n = f * MJ + (j + 1)
                            dve.wait_ge(sq_done, n)
                            dve.tensor_scalar(g_poly[:, :], g_sq[:, :], GELU_A, 1.0, ALU.mult, ALU.add).then_inc(poly_done, 1)
                            dve.wait_ge(poly_done, n)
                            dve.tensor_tensor(g_arg[:, :], bank[GATE_[j % 2]][:, :], g_poly[:, :], ALU.mult).then_inc(arg_done, 1)
                        if s % 3 == 1 and 4 <= s < 4 + 3 * MJ:
                            j = s // 3 - 1
                            n = f * MJ + (j + 1)
                            dve.wait_ge(tanh_done, n)
                            dve.scalar_tensor_tensor(out=g_lin[:, :], in0=g_tanh[:, :], scalar=1.0, in1=bank[GATE_[j % 2]][:, :],
                                                     op0=ALU.add, op1=ALU.mult).then_inc(lin_done, 1)
                            dve.wait_ge(lin_done, n)
                            dve.wait_ge(up_mm, n)
                            if not (isinstance(f, int) and f == 0 and j < 2):
                                dve.wait_ge(down_mm, f * MJ + max(j - 1, 0))
                            dve.scalar_tensor_tensor(out=inter[j % 2][:, :], in0=g_lin[:, :], scalar=0.5,
                                                     in1=bank[UP_[j % 2]][:, :], op0=ALU.mult,
                                                     op1=ALU.mult).then_inc(inter_done, 1)
                if mlp:
                    dve.wait_ge(down_mm, f * MJ + MJ)
                    if not (isinstance(f, int) and f == 0):
                        dve.wait_ge(tr_mm, f)
                    for o in range(KT):
                        last = dve.tensor_tensor(fin[:, o, :, :].rearrange("p b t -> p t b"),
                                                 bank[DOWN_][:, o * TOK:(o + 1) * TOK].rearrange("p (t b) -> p t b", b=B),
                                                 x2T[:, o, bass.ds(f * STEPS, STEPS), :], ALU.add)
                    last.then_inc(fin_done, 1)

            chunks(dve, chunk)


_INS = ['x', 'cond_2048', 'L0_cond_rms_weight', 'L0_cond_Wk', 'L0_cond_Wo', 'L0_cond_ln_gamma', 'L0_cond_ln_beta',
        'L0_attn_Wq', 'L0_attn_Wk', 'L0_attn_Wv', 'L0_attn_Wo', 'L0_attn_lambda_init',
        'L0_cond2_W_ih', 'L0_cond2_W_hh', 'L0_cond2_b_ih', 'L0_cond2_b_hh',
        'L0_ffn_gate_W_packed', 'L0_ffn_gate_scales', 'L0_ffn_up_W_packed', 'L0_ffn_up_scales',
        'L0_ffn_down_W_packed', 'L0_ffn_down_scales']
_OUTS = [((8, 128, 256), 'float32')]


def kernel(**inputs):
    import numpy as _np
    import concourse.bacc as _bacc
    from concourse import mybir as _mybir
    from concourse.bass_utils import run_bass_kernel_spmd as _run

    nc = _bacc.Bacc("TRN2", target_bir_lowering=False, num_devices=1)
    arrays, args = {}, []
    for name in _INS:
        a = _np.ascontiguousarray(inputs[name])
        arrays[f"in_{name}_dram"] = a
        args.append(nc.dram_tensor(f"in_{name}_dram", a.shape, _mybir.dt.from_np(a.dtype), kind="ExternalInput").ap())
    for i, (shape, dtype) in enumerate(_OUTS):
        dt = _mybir.dt.from_np(_np.dtype(dtype))
        args.append(nc.dram_tensor(f"out_{i}_dram", shape, dt, kind="ExternalOutput").ap())
    build(nc, *args)
    r = _run(nc, [arrays], core_ids=[0])
    got = tuple(r.results[0][f"out_{i}_dram"] for i in range(len(_OUTS)))
    return got[0]
```

```python
from contextlib import ExitStack

import numpy as np

import concourse.bass as bass
from concourse import mybir

F32 = mybir.dt.float32
BF16 = mybir.dt.bfloat16
I32 = mybir.dt.int32
ALU = mybir.AluOpType
ACT = mybir.ActivationFunctionType
AX = mybir.AxisListType.X

P = 128
B, T, D = 8, 128, 256
KT = D // P
NBLK = 8
BLK = T // NBLK
H = 16
HD = 128
HHD = HD // 2
SCALE = 1.0 / float(np.sqrt(HHD))
GB = 4
NG = B // GB
UNITS = NG * H
PAIRS = UNITS // 2
W4 = GB * T
MLP = 2048
MT = MLP // P
QB = 32
PK = 3 * P
NQ = 2 * PK // QB
GATES = 3 * D
STEPS = 16
CHUNKS = T // STEPS
QD = 32
NQD = P // QD
FQ = D // NQD
TOK = STEPS * B
NJ = 4
MJ = MT // NJ
EPS_RMS = 1e-6
EPS_LN = 1e-6
MASKED = -1e30
GELU_A = 0.044715
GELU_C = 0.7978845608028654


def build(nc, x, cond, rms_weight, Wk_c, Wo_c, ln_gamma, ln_beta, Wq, Wk, Wv, Wo, lambda_init,
          W_ih, W_hh, b_ih, b_hh, gate_W, gate_s, up_W, up_s, down_W, down_s, out):
    ctx = ExitStack()
    with ctx:
        def sb(name, shape, dt=F32):
            return ctx.enter_context(nc.sbuf_tensor(name, shape, dt))

        def sem(name):
            return ctx.enter_context(nc.semaphore(name))

        bank = [ctx.enter_context(nc.psum_tensor(f"bank{i}", [P, 512], F32)) for i in range(8)]

        ident = sb("ident", [P, P])
        ident_h = sb("ident_h", [P, P], BF16)
        mask = sb("mask", [P, GB, T], BF16)
        block_of = sb("block_of", [P, NBLK])
        batch_of = sb("batch_of", [B, B, P])
        ones_row = sb("ones_row", [1, P])
        pick = sb("pick", [P, P + QD])

        x_sb = sb("x_sb", [P, B, D])
        xn = sb("xn", [P, B, D])
        wk_c = sb("wk_c", [P, KT, D])
        wo_c = sb("wo_c", [P, KT, D])
        wkT_c = sb("wkT_c", [P, KT, D])
        woT_c = sb("woT_c", [P, KT, D])
        gamma = sb("gamma", [P, KT])
        beta = sb("beta", [P, KT])
        rmsw_b = sb("rmsw_b", [B * NBLK, D])
        query_b = sb("query_b", [B * NBLK, D])
        wquery = sb("wquery", [B * NBLK, D])
        blocksT = sb("blocksT", [P, KT, B * NBLK])
        junk64 = sb("junk64", [B * NBLK, D])
        junk64a = sb("junk64a", [B * NBLK, D])
        dot = sb("dot", [B * NBLK, 1])
        ssq = sb("ssq", [B * NBLK, 1])
        ms = sb("ms", [B * NBLK, 1])
        rms = sb("rms", [B * NBLK, 1])
        rrms = sb("rrms", [B * NBLK, 1])
        score_c = sb("score_c", [B * NBLK, 1])
        row_max = sb("row_max", [1, B])
        row_s = sb("row_s", [1, B, NBLK])
        row_e = sb("row_e", [1, B, NBLK])
        row_sum = sb("row_sum", [1, B])
        row_r = sb("row_r", [1, B])
        row_p = sb("row_p", [1, B, NBLK])
        weighted = sb("weighted", [P, KT, B * NBLK])
        attendedT = sb("attendedT", [P, KT, B])
        proj = sb("proj", [B, D])
        stats = sb("stats", [P, B, 6])
        meanvar = sb("meanvar", [P, B, 2])
        var_e = sb("var_e", [P, B])
        std = sb("std", [P, B])
        rstd = sb("rstd", [P, B])
        xT = sb("xT", [P, KT, B, T])
        hT = sb("hT", [P, KT, B * T])
        lam = sb("lam", [P, H])
        lam_e = sb("lam_e", [P, H])
        lam_1 = sb("lam_1", [P, H])
        lam_r = sb("lam_r", [P, H])
        neg_lam = sb("neg_lam", [P, H])

        wqkv = [sb(f"wqkv{i}", [P, 3, KT, HD]) for i in range(2)]
        wo = [sb(f"wo{i}", [P, D]) for i in range(2)]
        qT = sb("qT", [P, W4])
        kT = sb("kT", [P, W4])
        v = [sb(f"v{i}", [P, GB, HD]) for i in range(2)]
        neg_max = sb("neg_max", [P, 2, GB])
        exps = sb("exps", [P, 2, GB, T])
        sums = sb("sums", [P, 2, GB])
        rsums = sb("rsums", [P, 2, GB])
        coef2 = sb("coef2", [P, GB])
        probs1 = sb("probs1", [P, GB, T])
        diff = sb("diff", [P, GB, T])
        diffT = sb("diffT", [P, W4])
        attT = sb("attT", [P, W4])
        x2T = sb("x2T", [P, KT, T, B])
        packed = sb("packed", [P, 3, P], I32)
        scales = sb("scales", [P, NQ])
        code = sb("code", [P, PK, 2], I32)
        sign = sb("sign", [P, PK, 2], I32)
        line2 = sb("line2", [P, PK, 2])
        line3 = sb("line3", [P, PK, 2])
        mag = sb("mag", [P, PK, 2])
        value = sb("value", [P, PK, 2])
        wscaled = sb("wscaled", [P, NQ, QB])
        wguT = sb("wguT", [P, 2 * KT, MLP])
        wdT = sb("wdT", [P, MT, D])

        wih = sb("wih", [P, KT, GATES])
        whh = sb("whh", [P, KT, GATES])
        gate_bias = sb("gate_bias", [P, GATES])
        bias_h = sb("bias_h", [P, 2 * D])
        x_chunk = sb("x_chunk", [P, KT, TOK])
        gates = sb("gates", [P, 4, D])
        gates_next = sb("gates_next", [P, 3, D])
        h_row = sb("h_row", [P, FQ])
        ring = sb("ring", [P, STEPS, KT, QD])
        hchunk = sb("hchunk", [P, KT, TOK])
        rz = sb("rz", [P, 2 * FQ])
        n_g = sb("n_g", [P, FQ])
        r_hn = sb("r_hn", [P, FQ])
        n_pre = sb("n_pre", [P, FQ])
        zc = sb("zc", [P, FQ])
        zh = sb("zh", [P, FQ])
        zn = sb("zn", [P, FQ])
        mlp_a = x_sb.rearrange("p b d -> p (b d)")
        mlp_b = xn.rearrange("p b d -> p (b d)")
        g_sq, g_poly, g_arg, g_tanh = (mlp_a[:, i * 512:(i + 1) * 512] for i in range(4))
        g_lin = mlp_b[:, 0:512]
        inter = [mlp_b[:, (i + 1) * 512:(i + 2) * 512] for i in range(2)]
        fin = sb("fin", [P, KT, B, STEPS])
        out_sb = sb("out_sb", [P, D])

        x_in = [sem(f"x_in{i}") for i in range(2)]
        wc_in, row_in, gru_in = sem("wc_in"), sem("row_in"), sem("gru_in")
        consts = sem("consts")
        pool_zero = sem("pool_zero")
        wcT_mm, wcT_ev_v, wcT_ev_a = sem("wcT_mm"), sem("wcT_ev_v"), sem("wcT_ev_a")
        blocks_mm, blocks_ev = sem("blocks_mm"), sem("blocks_ev")
        dot_done, h_ready = sem("dot_done"), sem("h_ready")
        xT_mm, xT_ev = sem("xT_mm"), sem("xT_ev")
        keys_mm, ssq_done, rms_done = sem("keys_mm"), sem("ssq_done"), sem("rms_done")
        ms_done, score_done, score_mm = sem("ms_done"), sem("score_done"), sem("score_mm")
        rows_done, rexp_done, probs_done = sem("rows_done"), sem("rexp_done"), sem("probs_done")
        bcast_mm, att_done, proj_mm, proj_ev = sem("bcast_mm"), sem("att_done"), sem("proj_mm"), sem("proj_ev")
        projb_mm, var_done, std_done, xn_done = sem("projb_mm"), sem("var_done"), sem("std_done"), sem("xn_done")
        hT_mm, hT_ev = sem("hT_mm"), sem("hT_ev")
        lam_exp, lam_done = sem("lam_exp"), sem("lam_done")
        dve1 = sem("dve1")
        wqkv_in = [sem(f"wqkv_in{i}") for i in range(2)]
        wo_in = [sem(f"wo_in{i}") for i in range(2)]
        packed_in = sem("packed_in")
        q_mm, k_mm, v_mm, s_mm = sem("q_mm"), sem("k_mm"), sem("v_mm"), sem("s_mm")
        t_mm, wo_mm, o_mm = sem("t_mm"), sem("wo_mm"), sem("o_mm")
        q_ev, k_ev, v_ev, t_ev, o_ev = sem("q_ev"), sem("k_ev"), sem("v_ev"), sem("t_ev"), sem("o_ev")
        max_done, exp_done = sem("max_done"), sem("exp_done")
        rsum_done, coef_done, diff_done = sem("rsum_done"), sem("coef_done"), sem("diff_done")
        bits_done, lines_done, mag_done = sem("bits_done"), sem("lines_done"), sem("mag_done")
        value_done, wscaled_done, deq_mm, deq_ev = sem("value_done"), sem("wscaled_done"), sem("deq_mm"), sem("deq_ev")
        y_ev = sem("y_ev")
        step_mm, rz_act, n_act = sem("step_mm"), sem("rz_act"), sem("n_act")
        rhn_done, npre_done, zc_done, zn_done = sem("rhn_done"), sem("npre_done"), sem("zc_done"), sem("zn_done")
        hrow_done, h_zero, ab_in = sem("hrow_done"), sem("h_zero"), sem("ab_in")
        x_chunk_done, gates_mm, gates_ev = sem("x_chunk_done"), sem("gates_mm"), sem("gates_ev")
        gates_used, gates_moved = sem("gates_used"), sem("gates_moved")
        hchunk_done = sem("hchunk_done")
        gate_mm, up_mm, down_mm = sem("gate_mm"), sem("up_mm"), sem("down_mm")
        sq_done, poly_done, arg_done, tanh_done = sem("sq_done"), sem("poly_done"), sem("arg_done"), sem("tanh_done")
        lin_done, inter_done, fin_done = sem("lin_done"), sem("inter_done"), sem("fin_done")
        tr_mm, tr_ev, stored = sem("tr_mm"), sem("tr_ev"), sem("stored")

        def cols(b, n, k):
            return bank[b][:, 0:n * k].rearrange("p (n k) -> p n k", n=n)

        QB_, KB_, VB_, SB_, TO_, YB_ = 0, 1, 2, (3, 4), 5, (6, 7)
        STEP_, GATE_, UP_, DOWN_, TR_ = (0, 1), (2, 3), (4, 5), 6, 7
        n_rows = 3

        block = ctx.enter_context(nc.Block())

        def attention(eng, step):
            for g in range(NG):
                first, last = g * H // 2, (g + 1) * H // 2 - 1
                for p in (first,):
                    for par in range(2):
                        step(p, 2 * p + par, par, g)
                with eng.Fori(first + 1, last) as p:
                    for par in range(2):
                        step(p, p * 2 + par, par, g)
                for par in range(2):
                    step(last, 2 * last + par, par, g)

        def chunks(eng, chunk):
            chunk(0, True, False, True)
            chunk(1, True, True, True)
            with eng.Fori(2, CHUNKS - 1) as c:
                chunk(c, True, True, True)
            chunk(CHUNKS - 1, True, True, False)
            chunk(CHUNKS, False, True, False)

        @block.sync
        def _(sp):
            x_src = x.rearrange("b t d -> t b d")
            for i in range(2):
                sp.dma_start(x_sb[:, i * GB:(i + 1) * GB, :], x_src[:, i * GB:(i + 1) * GB, :]).then_inc(x_in[i], 16)

            def load_wqkv(u, par, h):
                if not (isinstance(u, int) and u < 2):
                    sp.wait_ge(v_mm, u - 1)
                for i, w in enumerate((Wq, Wk, Wv)):
                    src = w.rearrange("(k p) n -> p k n", p=P)
                    sp.dma_start(wqkv[par][:, i, :, :], src[:, :, bass.ds(h * HD, HD)]).then_inc(wqkv_in[par], 16)

            def load_wo(u, par, h):
                if not (isinstance(u, int) and u < 2):
                    sp.wait_ge(wo_mm, u - 1)
                sp.dma_start(wo[par][:, :], Wo[bass.ds(h * HD, HD), :]).then_inc(wo_in[par], 16)

            def load_packed(p):
                if not (isinstance(p, int) and p < 1):
                    sp.wait_ge(wscaled_done, p)
                sp.dma_start(packed[:, 0, :], gate_W[bass.ds(p * P, P), :]).then_inc(packed_in, 16)
                sp.dma_start(packed[:, 1, :], up_W[bass.ds(p * P, P), :]).then_inc(packed_in, 16)
                sp.dma_start(packed[:, 2, :].rearrange("p (k m) -> p k m", k=KT),
                             down_W.rearrange("(k p) m -> p k m", p=P)[:, :, bass.ds(p * (P // 2), P // 2)]).then_inc(packed_in, 16)
                sp.dma_start(scales[:, 0:8], gate_s[bass.ds(p * P, P), :]).then_inc(packed_in, 16)
                sp.dma_start(scales[:, 8:16], up_s[bass.ds(p * P, P), :]).then_inc(packed_in, 16)
                sp.dma_start(scales[:, 16:24].rearrange("p (k m) -> p k m", k=KT),
                             down_s.rearrange("(k p) m -> p k m", p=P)[:, :, bass.ds(p * 4, 4)]).then_inc(packed_in, 16)

            load_wqkv(0, 0, 0)
            load_packed(0)
            sp.dma_start(wih[:, :, :], W_ih.rearrange("(k p) n -> p k n", p=P)).then_inc(gru_in, 16)
            b_ih_row, b_hh_row = (b.rearrange("(a n) -> a n", a=1) for b in (b_ih, b_hh))
            sp.dma_start(gate_bias[:, :], b_ih_row.broadcast_to([P, GATES])).then_inc(gru_in, 16)
            sp.dma_start(bias_h[:, :], b_hh_row[:, 0:2 * D].broadcast_to([P, 2 * D])).then_inc(gru_in, 16)
            sp.dma_start(gates[:, 2, :], b_hh_row[:, 2 * D:GATES].broadcast_to([P, D])).then_inc(gru_in, 16)
            sp.wait_ge(h_zero, 1)
            for j in range(NQD):
                sp.dma_start(whh[j * QD:(j + 1) * QD, :, :],
                             W_hh[j * FQ:(j + 1) * FQ, :].rearrange("(k i) n -> i k n", i=QD)).then_inc(gru_in, 16)
                sp.dma_start(h_row[j * QD:j * QD + B, :], cond[:, j * FQ:(j + 1) * FQ]).then_inc(gru_in, 16)

            def step(p, u, par, g):
                h = u - g * H
                if isinstance(u, int) and h == H - 1:
                    if g < NG - 1:
                        load_wqkv(u + 1, 1 - par, 0)
                else:
                    load_wqkv(u + 1, 1 - par, h + 1)
                load_wo(u, par, h)
                if par == 1 and not (isinstance(p, int) and p == PAIRS - 1):
                    load_packed(p + 1)

            attention(sp, step)

            def store(c, gru, mlp, more):
                if not mlp:
                    return
                sp.wait_ge(tr_ev, c)
                sp.dma_start(out[:, bass.ds((c - 1) * STEPS, STEPS), :],
                             out_sb[:, :]).then_inc(stored, 16)

            chunks(sp, store)
            sp.wait_ge(stored, 16 * CHUNKS)

        @block.gpsimd
        def _(pool):
            pool.memset(ident[:, :], 0.0).then_inc(pool_zero, 1)
            pool.memset(mask[:, :, :], 0.0).then_inc(pool_zero, 1)
            pool.memset(block_of[:, :], 1.0).then_inc(pool_zero, 1)
            pool.memset(batch_of[:, :, :], 0.0).then_inc(pool_zero, 1)
            pool.memset(pick[:, :], 0.0).then_inc(pool_zero, 1)
            pool.memset(h_row[:, :], 0.0).then_inc(h_zero, 1)
            pool.memset(ones_row[:, :], 1.0).then_inc(consts, 1)
            pool.wait_ge(pool_zero, 5)
            pool.affine_select(out=ident[:, :], in_=ident[:, :], compare_op=ALU.not_equal, fill=1.0, base=0,
                               pattern=[[-1, P]], channel_multiplier=1).then_inc(pool_zero, 1)
            pool.affine_select(out=mask[:, :, :], in_=mask[:, :, :], compare_op=ALU.is_ge, fill=MASKED, base=0,
                               pattern=[[0, GB], [-1, T]], channel_multiplier=1).then_inc(consts, 1)
            pool.affine_select(out=block_of[:, :], in_=block_of[:, :], compare_op=ALU.is_ge, fill=0.0, base=0,
                               pattern=[[-BLK, NBLK]], channel_multiplier=1).then_inc(pool_zero, 1)
            pool.affine_select(out=batch_of[:, :, :], in_=batch_of[:, :, :], compare_op=ALU.not_equal, fill=1.0,
                               base=0, pattern=[[-1, B], [0, P]], channel_multiplier=1).then_inc(consts, 1)
            pool.affine_select(out=pick[:, :], in_=pick[:, :], compare_op=ALU.not_equal, fill=1.0, base=0,
                               pattern=[[-1, P + QD]], channel_multiplier=1).then_inc(consts, 1)
            pool.wait_ge(pool_zero, 7)
            pool.tensor_copy(ident_h[:, :], ident[:, :]).then_inc(consts, 1)
            pool.affine_select(out=block_of[:, :], in_=block_of[:, :], compare_op=ALU.is_ge, fill=0.0,
                               base=BLK - 1, pattern=[[BLK, NBLK]], channel_multiplier=-1).then_inc(consts, 1)

        NCONST = 6
        NGRU = 4 + 2 * NQD

        @block.tensor
        def _(pe):
            pe.wait_ge(consts, NCONST)
            pe.wait_ge(wc_in, 32)
            for i, (w, b) in enumerate(((wk_c, 0), (wo_c, 1))):
                dst = cols(b, KT, D)
                for c in range(KT):
                    for r in range(KT):
                        last = pe.transpose(dst[:, c, r * P:(r + 1) * P], w[:, r, c * P:(c + 1) * P], ident[:, :])
                last.then_inc(wcT_mm, 1)
            blk = bank[2][:, 0:KT * B * NBLK].rearrange("p (k b n) -> p k b n", k=KT, b=B)
            for b in range(B):
                if b % GB == 0:
                    pe.wait_ge(x_in[b // GB], 16)
                for k in range(KT):
                    last = pe.matmul(blk[:, k, b, :], x_sb[:, b, k * P:(k + 1) * P], block_of[:, :],
                                     start=True, stop=True)
            last.then_inc(blocks_mm, 1)
            pe.wait_ge(blocks_ev, 1)
            pe.wait_ge(wcT_ev_v, 1)
            for k in range(KT):
                last = pe.matmul(bank[3][0:B * NBLK, 0:D], blocksT[:, k, :], wkT_c[:, k, :],
                                 start=(k == 0), stop=(k == KT - 1))
            last.then_inc(keys_mm, 1)
            for b in range(B):
                for k in range(KT):
                    n = (k * B + b)
                    last = pe.transpose(bank[4 + n // 4][:, n % 4 * T:(n % 4 + 1) * T],
                                        x_sb[:, b, k * P:(k + 1) * P], ident[:, :])
            last.then_inc(xT_mm, 1)
            pe.wait_ge(score_done, 1)
            pe.transpose(bank[3][0:1, 256:256 + B * NBLK], score_c[:, :], ident[0:B * NBLK, 0:B * NBLK]).then_inc(score_mm, 1)
            pe.wait_ge(probs_done, 1)
            pe.matmul(bank[0][:, 0:B * NBLK], ones_row[:, :], row_p.rearrange("a b n -> a (b n)"),
                      start=True, stop=True).then_inc(bcast_mm, 1)
            pe.wait_ge(att_done, 1)
            pe.wait_ge(wcT_ev_a, 1)
            for k in range(KT):
                last = pe.matmul(bank[1][0:B, 0:D], attendedT[:, k, :], woT_c[:, k, :],
                                 start=(k == 0), stop=(k == KT - 1))
            last.then_inc(proj_mm, 1)
            pe.wait_ge(proj_ev, 1)
            pe.wait_ge(xT_ev, 4)
            for b in range(B):
                last = pe.matmul(cols(4 + b // 2, 2, D)[:, b % 2, :], batch_of[:, b, :], proj[:, :],
                                 start=True, stop=True)
                if b % 2:
                    last.then_inc(projb_mm, 1)
            for b in range(B):
                pe.wait_ge(xn_done, b + 1)
                for k in range(KT):
                    last = pe.transpose(bank[NG * k + b // GB][:, b % GB * T:(b % GB + 1) * T],
                                        xn[:, b, k * P:(k + 1) * P], ident[:, :])
                if b % GB == GB - 1:
                    last.then_inc(hT_mm, 1)
            pe.wait_ge(hT_ev, 4)
            pe.wait_ge(lam_done, 1)

            def project(p, u, par, g):
                w = wqkv[par]
                pe.wait_ge(wqkv_in[par], p * 48 + 48)
                for i, (b, done) in enumerate(((QB_, q_mm), (KB_, k_mm))):
                    for k in range(KT):
                        last = pe.matmul(bank[b][:, :], w[:, i, k, :], hT[:, k, g * W4:(g + 1) * W4],
                                         start=(k == 0), stop=(k == KT - 1))
                    last.then_inc(done, 1)
                if not (isinstance(u, int) and u == 0):
                    pe.wait_ge(v_ev, u)
                if not (isinstance(u, int) and u <= 2):
                    pe.wait_ge(deq_ev, 2 * (p - 1 + par))
                for b in range(GB):
                    for k in range(KT):
                        t0 = (g * GB + b) * T
                        last = pe.matmul(bank[VB_][:, b * HD:(b + 1) * HD], hT[:, k, t0:t0 + T], w[:, 2, k, :],
                                         start=(k == 0), stop=(k == KT - 1))
                last.then_inc(v_mm, 1)

            def turn_weights(p):
                pe.wait_ge(wscaled_done, p + 1)
                src = wscaled.rearrange("p n q -> p (n q)")
                for n in range(4):
                    last = pe.transpose(bank[TO_][:, n * P:(n + 1) * P], src[:, n * P:(n + 1) * P], ident[:, :])
                last.then_inc(deq_mm, 1)
                for n in range(2):
                    last = pe.transpose(bank[VB_][:, n * P:(n + 1) * P], src[:, (4 + n) * P:(5 + n) * P], ident[:, :])
                last.then_inc(deq_mm, 1)

            def project_out(u, par, start, stop):
                pe.wait_ge(wo_in[par], (u - par) * 8 + 16)
                pe.wait_ge(o_ev, u + 1)
                for f in range(KT):
                    last = pe.matmul(bank[YB_[f]][:, :], wo[par][:, f * P:(f + 1) * P], attT[:, :],
                                     start=start, stop=stop, skip_group_check=True)
                last.then_inc(wo_mm, 1)

            def step(p, u, par, g):
                at = u - g * H if isinstance(u, int) else -1
                if not (isinstance(u, int) and u == 0):
                    pe.wait_ge(o_ev, u)
                if par == 0 and not (isinstance(p, int) and p == 0):
                    pe.wait_ge(v_ev, u + 1)
                    turn_weights(p - 1)
                pe.wait_ge(q_ev, u + 1)
                pe.wait_ge(k_ev, u + 1)
                if not (isinstance(u, int) and u == 0):
                    pe.wait_ge(exp_done, u)
                for i in range(2):
                    pe.matmul(bank[SB_[i]][:, :], ident_h[:, :], mask.rearrange("p b s -> p (b s)"),
                              start=True, stop=False, skip_group_check=True)
                for b in range(GB):
                    for i in range(2):
                        rows = slice(i * HHD, (i + 1) * HHD)
                        last = pe.matmul(bank[SB_[i]][:, b * T:(b + 1) * T], qT[rows, b * T:(b + 1) * T],
                                         kT[rows, b * T:(b + 1) * T], start=False, stop=(b == GB - 1),
                                         skip_group_check=True)
                last.then_inc(s_mm, 1)
                if not (isinstance(u, int) and u == UNITS - 1):
                    project(p + par, u + 1, 1 - par, g + (at == H - 1))
                pe.wait_ge(diff_done, u + 1)
                if not (isinstance(p, int) and p == 0):
                    pe.wait_ge(deq_ev, 2 * p)
                for b in range(GB):
                    last = pe.transpose(bank[TO_][:, b * T:(b + 1) * T], diff[:, b, :], ident[:, :])
                last.then_inc(t_mm, 1)
                if not (isinstance(u, int) and u == 0):
                    if at == 1 and g > 0:
                        pe.wait_ge(y_ev, g)
                    project_out(u - 1, 1 - par, start=(at == 1), stop=(at == 0))
                pe.wait_ge(t_ev, u + 1)
                pe.wait_ge(v_ev, u + 1)
                for b in range(GB):
                    last = pe.matmul(bank[TO_][:, b * T:(b + 1) * T], v[par][:, b, :], diffT[:, b * T:(b + 1) * T],
                                     start=True, stop=True)
                last.then_inc(o_mm, 1)

            project(0, 0, 0, 0)
            attention(pe, step)
            project_out(UNITS - 1, 1, start=False, stop=True)
            turn_weights(PAIRS - 1)

            pe.wait_ge(gru_in, 16 * NGRU)
            pe.wait_ge(y_ev, NG)
            pe.wait_ge(deq_ev, 2 * PAIRS)

            def gates_in(c, part):
                n0, n1 = ((0, 2 * D), (2 * D, GATES))[part]
                pe.wait_ge(x_chunk_done, c + 1)
                if part == 1:
                    pe.wait_ge(gates_ev, 2 * c + 1)
                elif not (isinstance(c, int) and c <= 2):
                    pe.wait_ge(tr_ev, c - 2)
                for k in range(KT):
                    last = pe.matmul(bank[TR_][:, 0:n1 - n0], x_chunk[:, k, :], wih[:, k, n0:n1],
                                     start=(k == 0), stop=(k == KT - 1))
                last.then_inc(gates_mm, 1)

            def inputs_of(s):
                for j in range(NQD):
                    last = pe.matmul(bank[STEP_[s % 2]][j * QD:(j + 1) * QD, 0:4 * FQ], pick[:, s * B:s * B + QD],
                                     gates[:, :, j * FQ:(j + 1) * FQ], start=True, stop=False,
                                     skip_group_check=True, tile_position=(0, j * QD))
                if s == STEPS - 1:
                    last.then_inc(gates_used, 1)

            def recur(s):
                for k in range(KT):
                    for j in range(NQD):
                        last = pe.matmul(bank[STEP_[s % 2]][j * QD:(j + 1) * QD, 0:3 * FQ],
                                         ring[:, (s - 1) % STEPS, k, :],
                                         whh[:, k, :].rearrange("p (g f) -> p g f", g=3)[:, :, j * FQ:(j + 1) * FQ],
                                         start=False, stop=(k == KT - 1), skip_group_check=True,
                                         tile_position=(0, j * QD))
                last.then_inc(step_mm, 1)

            def hidden(f, j, up):
                if j == 0 and not up:
                    pe.wait_ge(hchunk_done, f + 1)
                if not up and not (isinstance(f, int) and f == 0 and j < 2):
                    pe.wait_ge(inter_done, f * MJ + max(j - 1, 0))
                dst = bank[(UP_ if up else GATE_)[j % 2]]
                for n in range(NJ):
                    m = NJ * j + n
                    for k in range(KT):
                        last = pe.matmul(dst[:, n * TOK:(n + 1) * TOK], wguT[:, (KT if up else 0) + k, m * P:(m + 1) * P],
                                         hchunk[:, k, :], start=(k == 0), stop=(k == KT - 1))
                last.then_inc(up_mm if up else gate_mm, 1)

            def down(f, j):
                pe.wait_ge(inter_done, f * MJ + (j + 1))
                if j == 0 and not (isinstance(f, int) and f == 0):
                    pe.wait_ge(fin_done, f)
                for n in range(NJ):
                    m = NJ * j + n
                    for o in range(KT):
                        last = pe.matmul(bank[DOWN_][:, o * TOK:(o + 1) * TOK], wdT[:, m, o * P:(o + 1) * P],
                                         inter[j % 2][:, n * TOK:(n + 1) * TOK], start=(m == 0 and o == 0),
                                         stop=(m == MT - 1), skip_group_check=True)
                last.then_inc(down_mm, 1)

            def turn_out(f, more):
                pe.wait_ge(fin_done, f + 1)
                if more:
                    pe.wait_ge(gates_ev, 2 * f + 6)
                elif not (isinstance(f, int) and f == 0):
                    pe.wait_ge(tr_ev, f)
                for o in range(KT):
                    last = pe.transpose(bank[TR_][:, o * P:(o + 1) * P],
                                        fin[:, o, :, :].rearrange("p b t -> p (b t)"), ident[:, :])
                last.then_inc(tr_mm, 1)

            def chunk(c, gru, mlp, more):
                f = c - 1
                for s in range(STEPS):
                    if gru:
                        pe.wait_ge(h_ready, c * STEPS + (s + 1))
                        recur(s)
                        if s < STEPS - 1:
                            inputs_of(s + 1)
                        elif more:
                            pe.wait_ge(gates_moved, c + 2)
                            inputs_of(0)
                        if s == 2 and more:
                            gates_in(c + 1, 0)
                        if s == 9 and more:
                            gates_in(c + 1, 1)
                    if mlp:
                        if s % 3 == 0 and s // 3 < MJ:
                            hidden(f, s // 3, False)
                        if s % 3 == 1 and s // 3 < MJ:
                            hidden(f, s // 3, True)
                        if s >= 5 and (s - 5) % 3 == 0:
                            down(f, (s - 5) // 3)
                if mlp:
                    turn_out(f, more)

            gates_in(0, 0)
            gates_in(0, 1)
            pe.wait_ge(gates_moved, 1)
            inputs_of(0)
            chunks(pe, chunk)

        @block.scalar
        def _(act):
            act.dma_start(wk_c[:, :, :], Wk_c.rearrange("(k p) n -> p k n", p=P)).then_inc(wc_in, 16)
            act.dma_start(wo_c[:, :, :], Wo_c.rearrange("(k p) n -> p k n", p=P)).then_inc(wc_in, 16)
            act.dma_start(rmsw_b[:, :], rms_weight.rearrange("(a n) -> a n", a=1).broadcast_to([B * NBLK, D])).then_inc(row_in, 16)
            act.dma_start(query_b[:, :], cond[1:2, :].broadcast_to([B * NBLK, D])).then_inc(row_in, 16)
            act.dma_start(lam[:, :], lambda_init.rearrange("(a n) -> a n", a=1).broadcast_to([P, H])).then_inc(row_in, 16)
            with nc.allow_non_contiguous_dma(reason="two short vectors onto partitions"):
                act.dma_start(gamma[:, :], ln_gamma.rearrange("(k p) -> p k", p=P)).then_inc(ab_in, 16)
                act.dma_start(beta[:, :], ln_beta.rearrange("(k p) -> p k", p=P)).then_inc(ab_in, 16)

            act.wait_ge(row_in, 16 * n_rows)
            act.activation(lam_e[:, :], lam[:, :], ACT.Exp, scale=-1.0).then_inc(lam_exp, 1)
            act.wait_ge(wcT_mm, 2)
            act.activation(woT_c[:, :, :], cols(1, KT, D), ACT.Copy).then_inc(wcT_ev_a, 1)
            act.wait_ge(dot_done, 1)
            act.activation(junk64a[:, :], bank[3][0:B * NBLK, 0:D], ACT.Square, accum_out=ssq[:, :]).then_inc(ssq_done, 1)
            act.wait_ge(xT_mm, 1)
            xT_flat = xT.rearrange("p k b t -> p (k b t)")
            for n in range(2):
                act.activation(xT_flat[:, n * 512:(n + 1) * 512], bank[4 + n][:, :], ACT.Copy).then_inc(xT_ev, 1)
            act.wait_ge(ms_done, 1)
            act.activation(rms[:, :], ms[:, :], ACT.Sqrt).then_inc(rms_done, 1)
            for n in range(2, 4):
                act.activation(xT_flat[:, n * 512:(n + 1) * 512], bank[4 + n][:, :], ACT.Copy).then_inc(xT_ev, 1)
            act.wait_ge(rows_done, 1)
            act.activation(row_e[:, :, :], row_s[:, :, :], ACT.Exp).then_inc(rexp_done, 1)
            act.wait_ge(var_done, 1)
            act.activation(std[:, :], var_e[:, :], ACT.Sqrt).then_inc(std_done, 1)
            act.wait_ge(ab_in, 32)
            for g in range(NG):
                act.wait_ge(hT_mm, g + 1)
                for k in range(KT):
                    act.activation(hT[:, k, g * W4:(g + 1) * W4], bank[NG * k + g][:, :], ACT.Identity,
                                   bias=beta[:, k:k + 1], scale=gamma[:, k:k + 1]).then_inc(hT_ev, 1)

            def keys_values(u, par):
                act.wait_ge(k_mm, u + 1)
                act.activation(kT[:, :], bank[KB_][:, :], ACT.Copy).then_inc(k_ev, 1)
                act.wait_ge(v_mm, u + 1)
                act.activation(v[par][:, :, :], cols(VB_, GB, HD), ACT.Copy).then_inc(v_ev, 1)

            def keep_weights(p):
                act.wait_ge(deq_mm, 2 * p + 1)
                act.activation(wguT[:, :, bass.ds(p * P, P)], cols(TO_, 2 * KT, P), ACT.Copy).then_inc(deq_ev, 1)
                act.wait_ge(deq_mm, 2 * p + 2)
                act.activation(wdT[:, bass.ds(p, 1), :].rearrange("p a d -> p (a d)"), bank[VB_][:, 0:D], ACT.Copy).then_inc(deq_ev, 1)

            def step(p, u, par, g):
                if par == 0 and not (isinstance(p, int) and p == 0):
                    keep_weights(p - 1)
                if not (isinstance(u, int) and u == 0):
                    act.wait_ge(diff_done, u)
                for i in range(2):
                    act.wait_ge(max_done, 2 * u + (i + 1))
                    for b in range(GB):
                        last = act.activation(exps[:, i, b, :], bank[SB_[i]][:, b * T:(b + 1) * T], ACT.Exp,
                                              bias=neg_max[:, i, b:b + 1], scale=1.0,
                                              accum_out=sums[:, i, b:b + 1])
                last.then_inc(exp_done, 1)
                if not (isinstance(u, int) and u == UNITS - 1):
                    keys_values(u + 1, 1 - par)
                act.wait_ge(t_mm, u + 1)
                act.activation(diffT[:, :], bank[TO_][:, :], ACT.Copy).then_inc(t_ev, 1)

            keys_values(0, 0)
            attention(act, step)
            keep_weights(PAIRS - 1)

            def move_gates(c):
                act.wait_ge(gates_ev, 2 * c + 2)
                if not (isinstance(c, int) and c == 0):
                    act.wait_ge(gates_used, c)
                act.activation(gates[:, 0:2, :], gates_next[:, 0:2, :], ACT.Copy)
                act.activation(gates[:, 3, :], gates_next[:, 2, :], ACT.Copy).then_inc(gates_moved, 1)

            act.wait_ge(gru_in, 16 * NGRU)
            move_gates(0)

            def chunk(c, gru, mlp, more):
                f = c - 1
                for s in range(STEPS):
                    if gru:
                        t = c * STEPS + s
                        act.wait_ge(step_mm, t + 1)
                        act.activation(rz[:, :], bank[STEP_[s % 2]][:, 0:2 * FQ], ACT.Sigmoid).then_inc(rz_act, 1)
                        act.wait_ge(npre_done, t + 1)
                        act.activation(n_g[:, :], n_pre[:, :], ACT.Tanh).then_inc(n_act, 1)
                        if s == STEPS - 2 and more:
                            move_gates(c + 1)
                    if mlp:
                        if s % 3 == 1 and s // 3 < MJ:
                            j = s // 3
                            act.wait_ge(gate_mm, f * MJ + (j + 1))
                            if not (isinstance(f, int) and f == 0 and j == 0):
                                act.wait_ge(poly_done, f * MJ + j)
                            act.activation(g_sq[:, :], bank[GATE_[j % 2]][:, :], ACT.Square).then_inc(sq_done, 1)
                        if s % 3 == 0 and 3 <= s < 3 + 3 * MJ:
                            j = s // 3 - 1
                            act.wait_ge(arg_done, f * MJ + (j + 1))
                            if not (isinstance(f, int) and f == 0 and j == 0):
                                act.wait_ge(lin_done, f * MJ + j)
                            act.activation(g_tanh[:, :], g_arg[:, :], ACT.Tanh, scale=GELU_C).then_inc(tanh_done, 1)
                if mlp:
                    act.wait_ge(tr_mm, f + 1)
                    if not (isinstance(f, int) and f == 0):
                        act.wait_ge(stored, 16 * f)
                    act.activation(out_sb[:, :], bank[TR_][:, 0:D], ACT.Copy).then_inc(tr_ev, 1)

            chunks(act, chunk)

        @block.vector
        def _(dve):
            mark = [0]

            def then(ins):
                mark[0] += 1
                ins.then_inc(dve1, 1)
                dve.wait_ge(dve1, mark[0])

            dve.wait_ge(row_in, 16 * n_rows)
            then(dve.tensor_tensor(wquery[:, :], rmsw_b[:, :], query_b[:, :], ALU.mult))
            dve.wait_ge(wcT_mm, 1)
            dve.tensor_copy(wkT_c[:, :, :], cols(0, KT, D)).then_inc(wcT_ev_v, 1)
            dve.wait_ge(blocks_mm, 1)
            dve.tensor_copy(blocksT[:, :, :], cols(2, KT, B * NBLK)).then_inc(blocks_ev, 1)
            dve.wait_ge(lam_exp, 1)
            then(dve.tensor_scalar(lam_1[:, :], lam_e[:, :], 1.0, None, ALU.add))
            then(dve.reciprocal(lam_r[:, :], lam_1[:, :]))
            dve.tensor_scalar(neg_lam[:, :], lam_r[:, :], -1.0, None, ALU.mult).then_inc(lam_done, 1)
            dve.wait_ge(keys_mm, 1)
            dve.scalar_tensor_tensor(out=junk64[:, :], in0=bank[3][0:B * NBLK, 0:D], scalar=1.0, in1=wquery[:, :],
                                     op0=ALU.mult, op1=ALU.mult, accum_out=dot[:, :]).then_inc(dot_done, 1)
            dve.wait_ge(ssq_done, 1)
            dve.tensor_scalar(ms[:, :], ssq[:, :], 1.0 / D, EPS_RMS, ALU.mult, ALU.add).then_inc(ms_done, 1)
            dve.wait_ge(rms_done, 1)
            then(dve.reciprocal(rrms[:, :], rms[:, :]))
            dve.tensor_tensor(score_c[:, :], dot[:, :], rrms[:, :], ALU.mult).then_inc(score_done, 1)
            dve.wait_ge(score_mm, 1)
            row = bank[3][0:1, 256:256 + B * NBLK].rearrange("p (b n) -> p b n", b=B)
            then(dve.tensor_reduce(row_max[:, :], row, AX, ALU.max))
            dve.tensor_tensor(row_s[:, :, :], row, row_max[:, :].unsqueeze(2).broadcast_to([1, B, NBLK]),
                              ALU.subtract).then_inc(rows_done, 1)
            dve.wait_ge(rexp_done, 1)
            then(dve.tensor_reduce(row_sum[:, :], row_e[:, :, :], AX, ALU.add))
            then(dve.reciprocal(row_r[:, :], row_sum[:, :]))
            dve.tensor_tensor(row_p[:, :, :], row_e[:, :, :], row_r[:, :].unsqueeze(2).broadcast_to([1, B, NBLK]),
                              ALU.mult).then_inc(probs_done, 1)
            dve.wait_ge(bcast_mm, 1)
            then(dve.tensor_tensor(weighted[:, :, :], blocksT[:, :, :],
                                   bank[0][:, 0:B * NBLK].unsqueeze(1).broadcast_to([P, KT, B * NBLK]), ALU.mult))
            dve.tensor_reduce(attendedT[:, :, :], weighted.rearrange("p k (b n) -> p k b n", b=B), AX,
                              ALU.add).then_inc(att_done, 1)
            dve.wait_ge(proj_mm, 1)
            dve.tensor_copy(proj[:, :], bank[1][0:B, 0:D]).then_inc(proj_ev, 1)
            for i in range(B // 2):
                dve.wait_ge(projb_mm, i + 1)
                last = dve.tensor_tensor(xn[:, 2 * i:2 * i + 2, :], x_sb[:, 2 * i:2 * i + 2, :], cols(4 + i, 2, D), ALU.add)
            then(last)
            for b in range(B):
                last = dve.bn_stats(stats[:, b, :], xn[:, b, :])
            then(last)
            for b in range(B):
                last = dve.bn_aggr(meanvar[:, b, :], stats[:, b, :])
            then(last)
            dve.tensor_scalar(var_e[:, :], meanvar[:, :, 1], EPS_LN, None, ALU.add).then_inc(var_done, 1)
            dve.wait_ge(std_done, 1)
            then(dve.reciprocal(rstd[:, :], std[:, :]))
            for b in range(B):
                dve.tensor_scalar(xn[:, b, :], xn[:, b, :], meanvar[:, b, 0:1], rstd[:, b:b + 1], ALU.subtract,
                                  ALU.mult).then_inc(xn_done, 1)

            def queries(u):
                dve.wait_ge(q_mm, u + 1)
                dve.tensor_scalar(qT[:, :], bank[QB_][:, :], SCALE, None, ALU.mult).then_inc(q_ev, 1)

            def codes(p):
                dve.wait_ge(packed_in, p * 96 + 96)
                src = packed.rearrange("p a n -> p (a n)")
                dve.tensor_scalar(code[:, :, 0], src, 7, None, ALU.bitwise_and).then_inc(bits_done, 1)
                dve.tensor_scalar(code[:, :, 1], src, 4, 7, ALU.logical_shift_right, ALU.bitwise_and).then_inc(bits_done, 1)
                dve.tensor_scalar(sign[:, :, 0], src, 8, 28, ALU.bitwise_and, ALU.logical_shift_left).then_inc(bits_done, 1)
                dve.tensor_scalar(sign[:, :, 1], src, 128, 24, ALU.bitwise_and, ALU.logical_shift_left).then_inc(bits_done, 1)

            def magnitudes(p):
                dve.wait_ge(bits_done, 4 * p + 4)
                dve.tensor_scalar(line2[:, :, :], code[:, :, :], 1.0, -2.0, ALU.mult, ALU.add).then_inc(lines_done, 1)
                dve.tensor_scalar(line3[:, :, :], code[:, :, :], 2.0, -8.0, ALU.mult, ALU.add).then_inc(lines_done, 1)
                dve.wait_ge(lines_done, 2 * p + 2)
                dve.scalar_tensor_tensor(out=mag[:, :, :], in0=code[:, :, :], scalar=0.5, in1=line2[:, :, :],
                                         op0=ALU.mult, op1=ALU.max).then_inc(mag_done, 1)
                dve.wait_ge(mag_done, 2 * p + 1)
                dve.tensor_tensor(mag[:, :, :], mag[:, :, :], line3[:, :, :], ALU.max).then_inc(mag_done, 1)

            def weights(p):
                dve.wait_ge(mag_done, 2 * p + 2)
                dve.tensor_tensor(value[:, :, :].bitcast(I32), mag[:, :, :].bitcast(I32), sign[:, :, :],
                                  ALU.bitwise_or).then_inc(value_done, 1)
                dve.wait_ge(value_done, p + 1)
                if not (isinstance(p, int) and p == 0):
                    dve.wait_ge(deq_mm, 2 * p)
                blocks = value.rearrange("p (n q) i -> p n (q i)", n=NQ)
                scale = scales[:, :].unsqueeze(2).broadcast_to([P, NQ, QB])
                nb = D // QB
                for a in range(2):
                    own = slice(a * nb, (a + 1) * nb)
                    dve.tensor_tensor(wscaled[:, own, :].rearrange("p (k j) q -> p j k q", k=KT),
                                      blocks[:, own, :].rearrange("p (j k) q -> p j k q", k=KT),
                                      scale[:, own, :].rearrange("p (j k) q -> p j k q", k=KT), ALU.mult)
                dve.tensor_tensor(wscaled[:, 2 * nb:, :], blocks[:, 2 * nb:, :], scale[:, 2 * nb:, :],
                                  ALU.mult).then_inc(wscaled_done, 1)

            def step(p, u, par, g):
                h = u - g * H
                dve.wait_ge(s_mm, u + 1)
                if not (isinstance(u, int) and u == 0):
                    dve.wait_ge(exp_done, u)
                for i in range(2):
                    dve.tensor_reduce(neg_max[:, i, :], cols(SB_[i], GB, T), AX, ALU.max, negate=True).then_inc(max_done, 1)
                if par == 0:
                    codes(p)
                else:
                    weights(p)
                dve.wait_ge(exp_done, u + 1)
                dve.reciprocal(rsums[:, :, :], sums[:, :, :]).then_inc(rsum_done, 1)
                dve.wait_ge(rsum_done, u + 1)
                dve.tensor_scalar(coef2[:, :], rsums[:, 1, :], neg_lam[:, bass.ds(h, 1)], None, ALU.mult).then_inc(coef_done, 1)
                for b in range(GB):
                    last = dve.tensor_scalar(probs1[:, b, :], exps[:, 0, b, :], rsums[:, 0, b:b + 1], None, ALU.mult)
                last.then_inc(coef_done, 1)
                dve.wait_ge(coef_done, 2 * u + 2)
                for b in range(GB):
                    last = dve.scalar_tensor_tensor(out=diff[:, b, :], in0=exps[:, 1, b, :], scalar=coef2[:, b:b + 1],
                                                    in1=probs1[:, b, :], op0=ALU.mult, op1=ALU.add)
                last.then_inc(diff_done, 1)
                if not (isinstance(u, int) and u == UNITS - 1):
                    queries(u + 1)
                if par == 0:
                    magnitudes(p)
                dve.wait_ge(o_mm, u + 1)
                dve.tensor_copy(attT[:, :], bank[TO_][:, :]).then_inc(o_ev, 1)
                if isinstance(u, int) and u == H:
                    residual(0)

            def residual(g):
                dve.wait_ge(wo_mm, (g + 1) * H)
                for k in range(KT):
                    last = dve.tensor_tensor(x2T[:, k, :, g * GB:(g + 1) * GB].rearrange("p t b -> p b t"),
                                             cols(YB_[k], GB, T), xT[:, k, g * GB:(g + 1) * GB, :], ALU.add)
                last.then_inc(y_ev, 1)

            queries(0)
            attention(dve, step)
            residual(1)

            dve.wait_ge(gru_in, 16 * NGRU)
            then(dve.tensor_tensor(gate_bias[:, 0:2 * D], gate_bias[:, 0:2 * D], bias_h[:, :], ALU.add))
            dve.transpose(ring[:, STEPS - 1, :, :].rearrange("p k q -> p (k q)"), h_row[:, :]).then_inc(h_ready, 1)

            def tokens(c):
                if not (isinstance(c, int) and c == 0):
                    dve.wait_ge(gates_mm, 2 * c)
                dve.tensor_copy(x_chunk.rearrange("p k (t b) -> p k t b", b=B),
                                x2T[:, :, bass.ds(c * STEPS, STEPS), :]).then_inc(x_chunk_done, 1)

            def gates_out(c, part):
                if part == 0 and not (isinstance(c, int) and c == 0):
                    dve.wait_ge(gates_moved, c)
                dve.wait_ge(gates_mm, 2 * c + (part + 1))
                if part == 0:
                    dve.tensor_tensor(gates_next[:, 0:2, :], cols(TR_, 2, D),
                                      gate_bias[:, 0:2 * D].rearrange("p (g f) -> p g f", g=2), ALU.add).then_inc(gates_ev, 1)
                else:
                    dve.tensor_tensor(gates_next[:, 2, :], bank[TR_][:, 0:D], gate_bias[:, 2 * D:GATES],
                                      ALU.add).then_inc(gates_ev, 1)

            dve.wait_ge(y_ev, NG)
            tokens(0)
            gates_out(0, 0)
            gates_out(0, 1)

            def chunk(c, gru, mlp, more):
                f = c - 1
                if mlp:
                    dve.wait_ge(h_ready, c * STEPS + 1)
                    if not (isinstance(f, int) and f == 0):
                        dve.wait_ge(up_mm, f * MJ)
                    for k in range(KT):
                        last = dve.tensor_copy(hchunk[:, k, :].rearrange("p (t b) -> p t b", b=B), ring[:, :, k, 0:B])
                    last.then_inc(hchunk_done, 1)
                if more:
                    tokens(c + 1)
                for s in range(STEPS):
                    if gru:
                        t = c * STEPS + s
                        step = bank[STEP_[s % 2]]
                        dve.wait_ge(rz_act, t + 1)
                        dve.tensor_tensor(r_hn[:, :], step[:, 2 * FQ:3 * FQ], rz[:, 0:FQ], ALU.mult).then_inc(rhn_done, 1)
                        dve.wait_ge(rhn_done, t + 1)
                        dve.tensor_tensor(n_pre[:, :], step[:, 3 * FQ:4 * FQ], r_hn[:, :], ALU.add).then_inc(npre_done, 1)
                        dve.tensor_scalar(zc[:, :], rz[:, FQ:], -1.0, 1.0, ALU.mult, ALU.add).then_inc(zc_done, 1)
                        dve.tensor_tensor(zh[:, :], rz[:, FQ:], h_row[:, :], ALU.mult)
                        dve.wait_ge(zc_done, t + 1)
                        dve.wait_ge(n_act, t + 1)
                        dve.tensor_tensor(zn[:, :], zc[:, :], n_g[:, :], ALU.mult).then_inc(zn_done, 1)
                        dve.wait_ge(zn_done, t + 1)
                        dve.tensor_tensor(h_row[:, :], zn[:, :], zh[:, :], ALU.add).then_inc(hrow_done, 1)
                        dve.wait_ge(hrow_done, t + 1)
                        dve.transpose(ring[:, s, :, :].rearrange("p k q -> p (k q)"), h_row[:, :]).then_inc(h_ready, 1)
                        if s == 3 and more:
                            gates_out(c + 1, 0)
                        if s == 12 and more:
                            gates_out(c + 1, 1)
                    if mlp:
                        if s % 3 == 2 and s // 3 < MJ:
                            j = s // 3
                            n = f * MJ + (j + 1)
                            dve.wait_ge(sq_done, n)
                            dve.tensor_scalar(g_poly[:, :], g_sq[:, :], GELU_A, 1.0, ALU.mult, ALU.add).then_inc(poly_done, 1)
                            dve.wait_ge(poly_done, n)
                            dve.tensor_tensor(g_arg[:, :], bank[GATE_[j % 2]][:, :], g_poly[:, :], ALU.mult).then_inc(arg_done, 1)
                        if s % 3 == 1 and 4 <= s < 4 + 3 * MJ:
                            j = s // 3 - 1
                            n = f * MJ + (j + 1)
                            dve.wait_ge(tanh_done, n)
                            dve.scalar_tensor_tensor(out=g_lin[:, :], in0=g_tanh[:, :], scalar=1.0, in1=bank[GATE_[j % 2]][:, :],
                                                     op0=ALU.add, op1=ALU.mult).then_inc(lin_done, 1)
                            dve.wait_ge(lin_done, n)
                            dve.wait_ge(up_mm, n)
                            if not (isinstance(f, int) and f == 0 and j < 2):
                                dve.wait_ge(down_mm, f * MJ + max(j - 1, 0))
                            dve.scalar_tensor_tensor(out=inter[j % 2][:, :], in0=g_lin[:, :], scalar=0.5,
                                                     in1=bank[UP_[j % 2]][:, :], op0=ALU.mult,
                                                     op1=ALU.mult).then_inc(inter_done, 1)
                if mlp:
                    dve.wait_ge(down_mm, f * MJ + MJ)
                    if not (isinstance(f, int) and f == 0):
                        dve.wait_ge(tr_mm, f)
                    for o in range(KT):
                        last = dve.tensor_tensor(fin[:, o, :, :].rearrange("p b t -> p t b"),
                                                 bank[DOWN_][:, o * TOK:(o + 1) * TOK].rearrange("p (t b) -> p t b", b=B),
                                                 x2T[:, o, bass.ds(f * STEPS, STEPS), :], ALU.add)
                    last.then_inc(fin_done, 1)

            chunks(dve, chunk)


_INS = ['x', 'cond_2048', 'L0_cond_rms_weight', 'L0_cond_Wk', 'L0_cond_Wo', 'L0_cond_ln_gamma', 'L0_cond_ln_beta',
        'L0_attn_Wq', 'L0_attn_Wk', 'L0_attn_Wv', 'L0_attn_Wo', 'L0_attn_lambda_init',
        'L0_cond2_W_ih', 'L0_cond2_W_hh', 'L0_cond2_b_ih', 'L0_cond2_b_hh',
        'L0_ffn_gate_W_packed', 'L0_ffn_gate_scales', 'L0_ffn_up_W_packed', 'L0_ffn_up_scales',
        'L0_ffn_down_W_packed', 'L0_ffn_down_scales']
_OUTS = [((8, 128, 256), 'float32')]


def kernel(**inputs):
    import numpy as _np
    import concourse.bacc as _bacc
    from concourse import mybir as _mybir
    from concourse.bass_utils import run_bass_kernel_spmd as _run

    nc = _bacc.Bacc("TRN2", target_bir_lowering=False, num_devices=1)
    arrays, args = {}, []
    for name in _INS:
        a = _np.ascontiguousarray(inputs[name])
        arrays[f"in_{name}_dram"] = a
        args.append(nc.dram_tensor(f"in_{name}_dram", a.shape, _mybir.dt.from_np(a.dtype), kind="ExternalInput").ap())
    for i, (shape, dtype) in enumerate(_OUTS):
        dt = _mybir.dt.from_np(_np.dtype(dtype))
        args.append(nc.dram_tensor(f"out_{i}_dram", shape, dt, kind="ExternalOutput").ap())
    build(nc, *args)
    r = _run(nc, [arrays], core_ids=[0])
    got = tuple(r.results[0][f"out_{i}_dram"] for i in range(len(_OUTS)))
    return got[0]
```

```python
from contextlib import ExitStack

import numpy as np

import concourse.bass as bass
from concourse import mybir

F32 = mybir.dt.float32
BF16 = mybir.dt.bfloat16
F32R = mybir.dt.float32r
I32 = mybir.dt.int32
ALU = mybir.AluOpType
ACT = mybir.ActivationFunctionType
AX = mybir.AxisListType.X

P = 128
B, T, D = 8, 128, 256
KT = D // P
NBLK = 8
BLK = T // NBLK
H = 16
HD = 128
HHD = HD // 2
SCALE = 1.0 / float(np.sqrt(HHD))
GB = 4
NG = B // GB
UNITS = NG * H
PAIRS = UNITS // 2
W4 = GB * T
MLP = 2048
MT = MLP // P
QB = 32
PK = 3 * P
NQ = 2 * PK // QB
GATES = 3 * D
STEPS = 16
CHUNKS = T // STEPS
QD = 32
NQD = P // QD
FQ = D // NQD
TOK = STEPS * B
NJ = 4
MJ = MT // NJ

BLOCKS = [("gate", 0), ("last", MJ - 1), ("up", 0), ("gate", 1), ("turn", 0), ("up", 1), ("in", 0), ("down", 0),
          ("in", 1), ("gate", 2), ("up", 2), ("down", 1), ("gate", 3), ("up", 3), ("down", 2)]
PIECES = {("in", 0): 2 * KT, ("in", 1): KT, ("turn", 0): 1}


def plan_slots():
    pieces = [(kind, j, i) for kind, j in BLOCKS for i in range(PIECES.get((kind, j), NJ * KT))]
    weights = [{"in": 9, "turn": 8}.get(kind, 4) for kind, j, i in pieces]
    slots, ends, done = [[] for _ in range(STEPS)], {}, 0
    for (kind, j, i), weight in zip(pieces, weights):
        slot = done * STEPS // sum(weights)
        slots[slot].append((kind, j, i))
        ends[kind, j] = slot
        done += weight
    return slots, ends


SLOTS, ENDS = plan_slots()
SQUARE_AT = [ENDS["gate", j] + 1 for j in range(MJ)]
TANH_AT = [max(SQUARE_AT[j] + 1, ENDS["up", j]) for j in range(MJ)]
GATES_AT = [ENDS["in", i] + 1 for i in range(2)]
INTER_AT = [min({at + 1, at + 2} - {*GATES_AT}) for at in TANH_AT]
FINISH_AT = ENDS["last", MJ - 1] + 1
ROWS_AT = ENDS["turn", 0]
HALF = STEPS // 2
EPS = 1e-6
MASKED = -1e30
GELU_A = 0.044715
GELU_C = 0.7978845608028654


def build(nc, x, cond, rms_weight, Wk_c, Wo_c, ln_gamma, ln_beta, Wq, Wk, Wv, Wo, lambda_init,
          W_ih, W_hh, b_ih, b_hh, gate_W, gate_s, up_W, up_s, down_W, down_s, out):
    ctx = ExitStack()
    with ctx:
        def sb(name, shape, dt=F32):
            return ctx.enter_context(nc.sbuf_tensor(name, shape, dt))

        def sem(name):
            return ctx.enter_context(nc.semaphore(name))

        bank = [ctx.enter_context(nc.psum_tensor(f"bank{i}", [P, 512], F32)) for i in range(8)]

        ident = sb("ident", [P, P])
        ident_h = sb("ident_h", [P, P], BF16)
        mask = sb("mask", [P, GB, T], BF16)
        batch_of = sb("batch_of", [B, B, P], F32R)
        ones_row = sb("ones_row", [1, P])

        x_at = nc.sbuf_base
        x_xn = sb("x_xn", [P, 2, B, D])
        x_sb, xn = x_xn[:, 0], x_xn[:, 1]
        wk_c = sb("wk_c", [P, KT, D])
        wo_c = sb("wo_c", [P, KT, D])
        wkT_c = sb("wkT_c", [P, KT, D])
        woT_c = sb("woT_c", [P, KT, D])
        gamma = sb("gamma", [P, KT])
        beta = sb("beta", [P, KT])
        rmsw_b = sb("rmsw_b", [B * NBLK, D])
        query_b = sb("query_b", [B * NBLK, D])
        wquery = sb("wquery", [B * NBLK, D])
        blocksT = sb("blocksT", [P, KT, B * NBLK])
        junk64 = sb("junk64", [B * NBLK, D])
        junk64a = sb("junk64a", [B * NBLK, D])
        dot = sb("dot", [B * NBLK, 1])
        ssq = sb("ssq", [B * NBLK, 1])
        rrms = sb("rrms", [B * NBLK, 1])
        score_c = sb("score_c", [B * NBLK, 1])
        row_max = sb("row_max", [1, B])
        row_s = sb("row_s", [1, B, NBLK])
        row_e = sb("row_e", [1, B, NBLK])
        row_sum = sb("row_sum", [1, B])
        row_r = sb("row_r", [1, B])
        row_p = sb("row_p", [1, B, NBLK])
        weighted = sb("weighted", [P, KT, B * NBLK])
        attendedT = sb("attendedT", [P, KT, B])
        proj_hi = sb("proj_hi", [B, D], F32R)
        proj_lo = sb("proj_lo", [B, D], F32R)
        stats = sb("stats", [P, B, 6])
        meanvar = sb("meanvar", [P, B, 2])
        rstd = sb("rstd", [P, B])
        eps = sb("eps", [P, 1])
        rms = sb("rms", [B * NBLK, 1])
        std = sb("std", [P, B])
        xT = sb("xT", [P, KT, B, T])
        hT = sb("hT", [P, KT, B * T])
        lam = sb("lam", [P, H])
        lam_e = sb("lam_e", [P, H])
        lam_1 = sb("lam_1", [P, H])
        lam_r = sb("lam_r", [P, H])
        neg_lam = sb("neg_lam", [P, H])

        wqk = [sb(f"wqk{i}", [P, 2, KT, HD]) for i in range(2)]
        wv = sb("wv", [P, KT, 2 * HD])
        wo = [sb(f"wo{i}", [P, D]) for i in range(2)]
        w_hi = sb("w_hi", [P, 2, KT, HD], F32R)
        w_lo = sb("w_lo", [P, 2, KT, HD], F32R)
        wo_hi = sb("wo_hi", [P, D], F32R)
        wo_lo = sb("wo_lo", [P, D], F32R)
        att_hi = sb("att_hi", [P, W4], F32R)
        att_lo = sb("att_lo", [P, W4], F32R)
        wv_hi = sb("wv_hi", [P, KT, 2 * HD], F32R)
        wv_lo = sb("wv_lo", [P, KT, 2 * HD], F32R)
        h_hi, h_lo = (nc.alloc_sbuf_tensor_at(name, [P, NG, KT, W4], F32R, offset=x_at + i * 4 * B * D)
                      for i, name in enumerate(("h_hi", "h_lo")))
        qT = sb("qT", [P, W4])
        kT = sb("kT", [P, W4])
        v = sb("v", [P, 2, GB, HD])
        neg_max = sb("neg_max", [P, 2, GB])
        exps = sb("exps", [P, 2, GB, T])
        batch_32 = exps.rearrange("p i b t -> p (i b t)")[0:B, 0:B * P].rearrange("p (b n) -> p b n", b=B)
        sums = sb("sums", [P, 2, GB])
        rsums = sb("rsums", [P, 2, GB])
        coef2 = sb("coef2", [P, GB])
        probs1 = sb("probs1", [P, GB, T])
        diff = sb("diff", [P, GB, T])
        diffT = sb("diffT", [P, W4])
        x2T = sb("x2T", [P, KT, T, B])
        packed = sb("packed", [P, 3, P], I32)
        scales = sb("scales", [P, NQ])
        code = sb("code", [P, PK, 2], I32)
        sign = sb("sign", [P, PK, 2], I32)
        line2 = sb("line2", [P, PK, 2])
        line3 = sb("line3", [P, PK, 2])
        mag = sb("mag", [P, PK, 2])
        value = sb("value", [P, PK, 2])
        wscaled = sb("wscaled", [P, NQ, QB])
        wguT = sb("wguT", [P, 2 * KT, MLP])
        wdT = sb("wdT", [P, MT, D])

        wih = sb("wih", [P, KT, GATES])
        whh = sb("whh", [P, KT, GATES])
        gate_bias = sb("gate_bias", [P, GATES])
        bias_h = sb("bias_h", [P, 2 * D])
        x_chunk = sb("x_chunk", [P, KT, TOK])
        gates_next = sb("gates_next", [P, NQD, 3 * FQ])
        gates = x_xn.rearrange("p a b d -> p (a b d)").rearrange("p (t f) -> p t f", t=STEPS)
        bias_hn = sb("bias_hn", [P, FQ])
        h_row = sb("h_row", [P, FQ])
        ring = sb("ring", [P, STEPS, KT, QD])
        hchunk = sb("hchunk", [P, KT, TOK])
        r_g = sb("r_g", [P, FQ])
        z_g = sb("z_g", [P, FQ])
        n_g = sb("n_g", [P, FQ])
        r_hn = sb("r_hn", [P, FQ])
        n_pre = sb("n_pre", [P, FQ])
        z_comp = sb("z_comp", [P, FQ])
        zh = sb("zh", [P, FQ])
        zn = sb("zn", [P, FQ])
        g_sq, g_arg, g_tanh, g_lin = (
            t.rearrange("p n i -> p (n i)")[:, 0:NJ * TOK] for t in (line2, line3, mag, value))
        inter = [qT[:, 0:NJ * TOK], kT[:, 0:NJ * TOK]]
        fin = sb("fin", [P, KT, B, STEPS])
        out_sb = sb("out_sb", [P, D])

        x_in = [sem(f"x_in{i}") for i in range(2)]
        wc_in, row_in, gru_in = sem("wc_in"), sem("row_in"), sem("gru_in")
        consts = sem("consts")
        pool_zero = sem("pool_zero")
        wcT_mm, wcT_ev = sem("wcT_mm"), sem("wcT_ev")
        blocks_done, eps_set = sem("blocks_done"), sem("eps_set")
        rms_done, var_done, std_done = sem("rms_done"), sem("var_done"), sem("std_done")
        wo_c_in, ssq_done, proj_hi_done, batch_done = sem("wo_c_in"), sem("ssq_done"), sem("proj_hi_done"), sem("batch_done")
        dot_done, h_ready = sem("dot_done"), sem("h_ready")
        xT_mm, xT_ev = sem("xT_mm"), sem("xT_ev")
        keys_mm = sem("keys_mm")
        score_done, score_mm = sem("score_done"), sem("score_mm")
        rows_done, rexp_done, probs_done = sem("rows_done"), sem("rexp_done"), sem("probs_done")
        bcast_mm, att_done, proj_mm, proj_ev = sem("bcast_mm"), sem("att_done"), sem("proj_mm"), sem("proj_ev")
        projb_mm, xn_done = sem("projb_mm"), sem("xn_done")
        hT_mm, hT_ev = sem("hT_mm"), sem("hT_ev")
        lam_exp = sem("lam_exp")
        dve1 = sem("dve1")
        wqk_in = [sem(f"wqk_in{i}") for i in range(2)]
        wv_in, wv_hi_done, wv_lo_done = sem("wv_in"), sem("wv_hi_done"), sem("wv_lo_done")
        wo_in = [sem(f"wo_in{i}") for i in range(2)]
        packed_in, scales_in, bias_in = sem("packed_in"), sem("scales_in"), sem("bias_in")
        q_mm, k_mm, v_mm, s_mm = sem("q_mm"), sem("k_mm"), sem("v_mm"), sem("s_mm")
        t_mm, wo_mm, o_mm = sem("t_mm"), sem("wo_mm"), sem("o_mm")
        wo_hi_done, wo_lo_done, o_hi = sem("wo_hi_done"), sem("wo_lo_done"), sem("o_hi")
        w_hi_done, w_lo_done, h_lo_done = sem("w_hi_done"), sem("w_lo_done"), sem("h_lo_done")
        q_ev, k_ev, v_ev, t_ev, o_ev = sem("q_ev"), sem("k_ev"), sem("v_ev"), sem("t_ev"), sem("o_ev")
        max_done, exp_done = sem("max_done"), sem("exp_done")
        rsum_done, coef_done, diff_done = sem("rsum_done"), sem("coef_done"), sem("diff_done")
        bits_done, lines_done, mag_done = sem("bits_done"), sem("lines_done"), sem("mag_done")
        value_done, wscaled_done, deq_mm, deq_ev = sem("value_done"), sem("wscaled_done"), sem("deq_mm"), sem("deq_ev")
        y_ev = sem("y_ev")
        rn_mm, z_mm, r_act, z_act, n_act = sem("rn_mm"), sem("z_mm"), sem("r_act"), sem("z_act"), sem("n_act")
        rhn_done, npre_done, zn_done = sem("rhn_done"), sem("npre_done"), sem("zn_done")
        hrow_done, h_zero, ab_in = sem("hrow_done"), sem("h_zero"), sem("ab_in")
        preset_rn, preset_z = sem("preset_rn"), sem("preset_z")
        half_in = [sem(f"half_in{i}") for i in range(2)]
        gates_set = sem("gates_set")
        x_chunk_done, gates_mm, gates_ev = sem("x_chunk_done"), sem("gates_mm"), sem("gates_ev")
        hchunk_done = sem("hchunk_done")
        gate_mm, up_mm, down_mm = sem("gate_mm"), sem("up_mm"), sem("down_mm")
        sq_done, arg_done, tanh_done = sem("sq_done"), sem("arg_done"), sem("tanh_done")
        lin_done, inter_done, fin_done = sem("lin_done"), sem("inter_done"), sem("fin_done")
        tr_mm, tr_ev, stored = sem("tr_mm"), sem("tr_ev"), sem("stored")

        def xT_bank(g, k):
            return bank[4 + NG * k + g]

        def hT_bank(g, k):
            return bank[(0, 2)[k] if g == 0 else YB_[k]]

        def cols(b, n, k):
            return bank[b][:, 0:n * k].rearrange("p (n k) -> p n k", n=n)

        QB_, KB_, VB_, SB_, TO_, YB_ = 0, 1, 2, (3, 4), 5, (6, 7)
        RN_, Z_, GATE_, UP_, DOWN_, TR_ = 0, 1, (2, 3), (4, 5), 6, 7
        n_rows = 3

        def gates_bank(c, part):
            return GATE_[0] if part == 1 and isinstance(c, int) and c == 0 else TR_

        block = ctx.enter_context(nc.Block())

        def attention(eng, step):
            for g in range(NG):
                first, last = g * H // 2, (g + 1) * H // 2 - 1
                for p in (first,):
                    for par in range(2):
                        step(p, 2 * p + par, par, g)
                with eng.Fori(first + 1, last) as p:
                    for par in range(2):
                        step(p, p * 2 + par, par, g)
                for par in range(2):
                    step(last, 2 * last + par, par, g)

        def chunks(eng, chunk):
            chunk(0, True, False, True, False)
            chunk(1, True, True, True, False)
            with eng.Fori(2, CHUNKS - 1) as c:
                chunk(c, True, True, True, True)
            chunk(CHUNKS - 1, True, True, False, True)
            chunk(CHUNKS, False, True, False, True)

        @block.sync
        def _(sp):
            x_src = x.rearrange("b t d -> t b d")
            for i in range(2):
                sp.dma_start(x_sb[:, i * GB:(i + 1) * GB, :], x_src[:, i * GB:(i + 1) * GB, :]).then_inc(x_in[i], 16)

            def load_wqk(u, par, h):
                if not (isinstance(u, int) and u < 2):
                    sp.wait_ge(w_lo_done, u - 1)
                for i, w in enumerate((Wq, Wk)):
                    src = w.rearrange("(k p) n -> p k n", p=P)
                    sp.dma_start(wqk[par][:, i, :, :], src[:, :, bass.ds(h * HD, HD)]).then_inc(wqk_in[par], 16)

            def load_wv(p, h):
                if not (isinstance(p, int) and p == 0):
                    sp.wait_ge(wv_lo_done, p)
                sp.dma_start(wv[:, :, :], Wv.rearrange("(k p) n -> p k n", p=P)[:, :, bass.ds(h * HD, 2 * HD)]).then_inc(wv_in, 16)

            def load_wo(u, par, h):
                if not (isinstance(u, int) and u < 2):
                    sp.wait_ge(wo_lo_done, u - 1)
                sp.dma_start(wo[par][:, :], Wo[bass.ds(h * HD, HD), :]).then_inc(wo_in[par], 16)

            def load_packed(p):
                if not (isinstance(p, int) and p < 1):
                    sp.wait_ge(bits_done, 4 * p)
                sp.dma_start(packed[:, 0, :], gate_W[bass.ds(p * P, P), :]).then_inc(packed_in, 16)
                sp.dma_start(packed[:, 1, :], up_W[bass.ds(p * P, P), :]).then_inc(packed_in, 16)
                sp.dma_start(packed[:, 2, :].rearrange("p (k m) -> p k m", k=KT),
                             down_W.rearrange("(k p) m -> p k m", p=P)[:, :, bass.ds(p * (P // 2), P // 2)]).then_inc(packed_in, 16)

            def load_scales(p):
                if not (isinstance(p, int) and p < 1):
                    sp.wait_ge(wscaled_done, p)
                sp.dma_start(scales[:, 0:8], gate_s[bass.ds(p * P, P), :]).then_inc(scales_in, 16)
                sp.dma_start(scales[:, 8:16], up_s[bass.ds(p * P, P), :]).then_inc(scales_in, 16)
                sp.dma_start(scales[:, 16:24].rearrange("p (k m) -> p k m", k=KT),
                             down_s.rearrange("(k p) m -> p k m", p=P)[:, :, bass.ds(p * 4, 4)]).then_inc(scales_in, 16)

            load_wqk(0, 0, 0)
            load_wv(0, 0)
            load_wqk(1, 1, 1)
            load_packed(0)
            load_scales(0)
            sp.dma_start(wih[:, :, :], W_ih.rearrange("(k p) n -> p k n", p=P)).then_inc(gru_in, 16)
            b_ih_row, b_hh_row = (b.rearrange("(a n) -> a n", a=1) for b in (b_ih, b_hh))
            sp.dma_start(gate_bias[:, :], b_ih_row.broadcast_to([P, GATES])).then_inc(gru_in, 16)
            sp.dma_start(bias_h[:, :], b_hh_row[:, 0:2 * D].broadcast_to([P, 2 * D])).then_inc(gru_in, 16)
            for j in range(NQD):
                n0 = 2 * D + j * FQ
                sp.dma_start(bias_hn[j * QD:(j + 1) * QD, :],
                             b_hh_row[:, n0:n0 + FQ].broadcast_to([QD, FQ])).then_inc(bias_in, 16)
            sp.wait_ge(h_zero, 1)
            for j in range(NQD):
                sp.dma_start(whh[j * QD:(j + 1) * QD, :, :],
                             W_hh[j * FQ:(j + 1) * FQ, :].rearrange("(k i) n -> i k n", i=QD)).then_inc(gru_in, 16)
                sp.dma_start(h_row[j * QD:j * QD + B, :], cond[:, j * FQ:(j + 1) * FQ]).then_inc(gru_in, 16)

            def step(p, u, par, g):
                h = u - g * H
                wraps = isinstance(u, int) and h >= H - 2
                if not wraps or g < NG - 1:
                    ahead = h + 2 - H if wraps else h + 2
                    load_wqk(u + 2, par, ahead)
                    if par == 0:
                        load_wv(p + 1, ahead)
                load_wo(u, par, h)
                if par == 0 and not (isinstance(p, int) and p == PAIRS - 1):
                    load_packed(p + 1)
                if par == 0 and not (isinstance(p, int) and p == 0):
                    load_scales(p)

            attention(sp, step)

            def load_gates(c, half):
                if isinstance(c, int) and c == 0:
                    sp.wait_ge(gates_set, 1)
                elif half == 0:
                    sp.wait_ge(preset_z, c * STEPS - HALF)
                else:
                    sp.wait_ge(preset_z, c * STEPS)
                sp.wait_ge(gates_ev, 2 * c + 2)
                rows = slice(half * HALF * B, (half + 1) * HALF * B)
                for j in range(NQD):
                    sp.dma_start(gates[j * QD:j * QD + B, half * HALF:(half + 1) * HALF, 0:3 * FQ],
                                 gates_next[rows, j, :]).then_inc(half_in[half], 16)

            load_gates(0, 0)
            load_gates(0, 1)

            def store(c, gru, mlp, more, end):
                if end:
                    store_chunk(c - 2)
                if more:
                    load_gates(c + 1, 0)
                    load_gates(c + 1, 1)

            def store_chunk(f):
                sp.wait_ge(tr_ev, f + 1)
                sp.dma_start(out[:, bass.ds(f * STEPS, STEPS), :], out_sb[:, :]).then_inc(stored, 16)

            chunks(sp, store)
            store_chunk(CHUNKS - 1)
            sp.wait_ge(stored, 16 * CHUNKS)

        @block.gpsimd
        def _(pool):
            pool.memset(ident[:, :], 0.0).then_inc(pool_zero, 1)
            pool.memset(mask[:, :, :], 0.0).then_inc(pool_zero, 1)
            pool.wait_ge(pool_zero, 1)
            pool.affine_select(out=ident[:, :], in_=ident[:, :], compare_op=ALU.not_equal, fill=1.0, base=0,
                               pattern=[[-1, P]], channel_multiplier=1).then_inc(consts, 1)
            pool.memset(batch_32, 0.0).then_inc(pool_zero, 1)
            pool.memset(h_row[:, :], 0.0).then_inc(h_zero, 1)
            pool.memset(ones_row[:, :], 1.0).then_inc(consts, 1)
            pool.memset(eps[:, :], EPS).then_inc(eps_set, 1)
            pool.wait_ge(pool_zero, 3)
            pool.affine_select(out=mask[:, :, :], in_=mask[:, :, :], compare_op=ALU.is_ge, fill=MASKED, base=0,
                               pattern=[[0, GB], [-1, T]], channel_multiplier=1).then_inc(consts, 1)
            pool.affine_select(out=batch_32, in_=batch_32, compare_op=ALU.not_equal, fill=1.0,
                               base=0, pattern=[[-1, B], [0, P]], channel_multiplier=1).then_inc(consts, 1)
            pool.wait_ge(consts, 4)
            pool.tensor_copy(ident_h[:, :], ident[:, :]).then_inc(consts, 1)

            def split_weights(u, par):
                pool.wait_ge(w_hi_done, u + 1)
                pool.tensor_tensor(w_lo[:, :, :, :], wqk[par][:, :, :, :], w_hi[:, :, :, :].bitcast(F32),
                                   ALU.subtract).then_inc(w_lo_done, 1)

            def split_value_weights(p):
                pool.wait_ge(wv_hi_done, p + 1)
                pool.tensor_tensor(wv_lo[:, :, :], wv[:, :, :], wv_hi[:, :, :].bitcast(F32), ALU.subtract).then_inc(wv_lo_done, 1)

            def step(p, u, par, g):
                if not (isinstance(u, int) and u >= UNITS - 2):
                    split_weights(u + 2, par)
                pool.wait_ge(wo_hi_done, u + 1)
                pool.tensor_tensor(wo_lo[:, :], wo[par][:, :], wo_hi[:, :].bitcast(F32), ALU.subtract).then_inc(wo_lo_done, 1)
                if par == 0 and not (isinstance(p, int) and p == PAIRS - 1):
                    split_value_weights(p + 1)

            split_weights(0, 0)
            split_value_weights(0)
            split_weights(1, 1)
            attention(pool, step)
            pool.wait_ge(k_mm, UNITS)
            pool.wait_ge(bias_in, 16 * NQD)
            pool.memset(gates[:, :, 0:3 * FQ], 0.0)
            pool.tensor_copy(gates[:, :, 3 * FQ:4 * FQ],
                             bias_hn[:, :].unsqueeze(1).broadcast_to([P, STEPS, FQ])).then_inc(gates_set, 1)

        NCONST = 5
        NGRU = 3 + 2 * NQD

        @block.tensor
        def _(pe):
            pe.wait_ge(consts, 1)
            for g in range(NG):
                pe.wait_ge(x_in[g], 16)
                for k in range(KT):
                    for b in range(GB):
                        last = pe.transpose(xT_bank(g, k)[:, b * T:(b + 1) * T],
                                            x_sb[:, g * GB + b, k * P:(k + 1) * P], ident[:, :])
                    last.then_inc(xT_mm, 1)
            for w, b, done_in in ((wk_c, 0, wc_in), (wo_c, 1, wo_c_in)):
                pe.wait_ge(done_in, 16)
                dst = cols(b, KT, D)
                for c in range(KT):
                    for r in range(KT):
                        last = pe.transpose(dst[:, c, r * P:(r + 1) * P], w[:, r, c * P:(c + 1) * P], ident[:, :])
                last.then_inc(wcT_mm, 1)
            def keep_warm(b, n):
                for _ in range(n):
                    pe.matmul(bank[b][:, :], ident_h[:, :], mask.rearrange("p b s -> p (b s)"), start=True, stop=True)

            pe.wait_ge(consts, NCONST)
            keep_warm(2, 3)
            pe.wait_ge(blocks_done, NG * KT)
            pe.wait_ge(wcT_ev, 1)
            for k in range(KT):
                last = pe.matmul(bank[3][0:B * NBLK, 0:D], blocksT[:, k, :], wkT_c[:, k, :],
                                 start=(k == 0), stop=(k == KT - 1))
            last.then_inc(keys_mm, 1)
            keep_warm(2, 8)
            pe.wait_ge(score_done, 1)
            pe.transpose(bank[3][0:1, 256:256 + B * NBLK], score_c[:, :], ident[0:B * NBLK, 0:B * NBLK]).then_inc(score_mm, 1)
            keep_warm(2, 6)
            pe.wait_ge(probs_done, 1)
            pe.matmul(bank[0][:, 0:B * NBLK], ones_row[:, :], row_p.rearrange("a b n -> a (b n)"),
                      start=True, stop=True).then_inc(bcast_mm, 1)
            keep_warm(2, 3)
            pe.wait_ge(att_done, 1)
            pe.wait_ge(wcT_ev, 2)
            for k in range(KT):
                last = pe.matmul(bank[1][0:B, 0:D], attendedT[:, k, :], woT_c[:, k, :],
                                 start=(k == 0), stop=(k == KT - 1))
            last.then_inc(proj_mm, 1)
            keep_warm(2, 4)
            pe.wait_ge(batch_done, 1)
            pe.wait_ge(proj_ev, 1)
            pe.wait_ge(xT_ev, 4)
            for b in range(B):
                for part in (proj_hi, proj_lo):
                    last = pe.matmul(cols(4 + b // 2, 2, D)[:, b % 2, :], batch_of[:, b, :], part[:, :],
                                     start=(part is proj_hi), stop=(part is proj_lo))
                if b % 2:
                    last.then_inc(projb_mm, 1)
            keep_warm(2, 14)

            def turn_norm(g):
                for b in range(GB):
                    pe.wait_ge(xn_done, g * GB + b + 1)
                    for k in range(KT):
                        last = pe.transpose(hT_bank(g, k)[:, b * T:(b + 1) * T],
                                            xn[:, g * GB + b, k * P:(k + 1) * P], ident[:, :])
                last.then_inc(hT_mm, 1)

            turn_norm(0)
            keep_warm(3, 9)

            def project(u, g):
                pe.wait_ge(w_lo_done, u + 1)
                for i, (b, done) in enumerate(((QB_, q_mm), (KB_, k_mm))):
                    for k in range(KT):
                        if isinstance(u, int) and u in (0, H) and i == 0:
                            pe.wait_ge(h_lo_done, g * KT + k + 1)
                        for n, (w_part, h_part) in enumerate(((w_hi, h_hi), (w_hi, h_lo), (w_lo, h_hi))):
                            last = pe.matmul(bank[b][:, :], w_part[:, i, k, :], h_part[:, g, k, :],
                                             start=(k == 0 and n == 0), stop=(k == KT - 1 and n == 2))
                    last.then_inc(done, 1)

            def project_values(p, g, half):
                if half == 0:
                    pe.wait_ge(wv_lo_done, p + 1)
                    if not (isinstance(p, int) and p == 0):
                        pe.wait_ge(v_ev, 2 * p)
                elif isinstance(p, int) and p == 0:
                    pe.wait_ge(v_ev, 1)
                else:
                    pe.wait_ge(deq_ev, 2 * p - 1)
                for b in range(GB // 2):
                    t0 = (half * GB // 2 + b) * T
                    for k in range(KT):
                        for n, (h_part, w_part) in enumerate(((h_hi, wv_hi), (h_hi, wv_lo), (h_lo, wv_hi))):
                            last = pe.matmul(cols(VB_, 2, 2 * HD)[:, b, :], h_part[:, g, k, t0:t0 + T], w_part[:, k, :],
                                             start=(k == 0 and n == 0), stop=(k == KT - 1 and n == 2))
                last.then_inc(v_mm, 1)

            def turn_weights(p):
                pe.wait_ge(wscaled_done, p + 1)
                src = wscaled.rearrange("p n q -> p (n q)")
                for n in range(2):
                    last = pe.transpose(bank[VB_][:, n * P:(n + 1) * P], src[:, (4 + n) * P:(5 + n) * P], ident[:, :])
                last.then_inc(deq_mm, 1)
                for n in range(4):
                    last = pe.transpose(bank[TO_][:, n * P:(n + 1) * P], src[:, n * P:(n + 1) * P], ident[:, :])
                last.then_inc(deq_mm, 1)

            def project_out(u, start, stop):
                pe.wait_ge(wo_lo_done, u + 1)
                pe.wait_ge(o_ev, u + 1)
                for f in range(KT):
                    for n, (w_part, o_part) in enumerate(((wo_hi, att_hi), (wo_hi, att_lo), (wo_lo, att_hi))):
                        last = pe.matmul(bank[YB_[f]][:, :], w_part[:, f * P:(f + 1) * P], o_part[:, :],
                                         start=(start and n == 0), stop=(stop and n == 2), skip_group_check=True)
                last.then_inc(wo_mm, 1)

            def turn_diff(u):
                for b in range(GB):
                    if b % 2 == 0:
                        pe.wait_ge(diff_done, 2 * u + (b // 2 + 1))
                    last = pe.transpose(bank[TO_][:, b * T:(b + 1) * T], diff[:, b, :], ident[:, :])
                last.then_inc(t_mm, 1)

            def attend(p, u, par):
                pe.wait_ge(t_ev, u + 1)
                pe.wait_ge(v_ev, p * 2 + 2)
                for b in range(GB):
                    last = pe.matmul(bank[TO_][:, b * T:(b + 1) * T], v[:, par, b, :], diffT[:, b * T:(b + 1) * T],
                                     start=True, stop=True)
                last.then_inc(o_mm, 1)

            def step(p, u, par, g):
                at = u - g * H if isinstance(u, int) else -1
                begun = not (isinstance(u, int) and u == 0)
                more = not (isinstance(u, int) and u == UNITS - 1)
                turned = par == 0 and not (isinstance(p, int) and p == 0)
                if begun:
                    if not (isinstance(p, int) and p + par <= 1):
                        pe.wait_ge(deq_ev, 2 * (p - 1 + par))
                    turn_diff(u - 1)
                pe.wait_ge(q_ev, u + 1)
                pe.wait_ge(k_ev, u + 1)
                if begun:
                    pe.wait_ge(exp_done, 2 * u)
                for i in range(2):
                    pe.matmul(bank[SB_[i]][:, :], ident_h[:, :], mask.rearrange("p b s -> p (b s)"),
                              start=True, stop=False, skip_group_check=True)
                for b in range(GB):
                    for i in range(2):
                        rows = slice(i * HHD, (i + 1) * HHD)
                        last = pe.matmul(bank[SB_[i]][:, b * T:(b + 1) * T], qT[rows, b * T:(b + 1) * T],
                                         kT[rows, b * T:(b + 1) * T], start=False, stop=(b == GB - 1),
                                         skip_group_check=True)
                last.then_inc(s_mm, 1)
                if begun:
                    attend(p - 1 + par, u - 1, 1 - par)
                if more:
                    project(u + 1, g + (at == H - 1))
                if isinstance(u, int) and u == 0:
                    turn_norm(1)
                if turned:
                    pe.wait_ge(v_ev, u + 1)
                    pe.wait_ge(o_ev, u)
                    turn_weights(p - 1)
                if begun:
                    if at == 1 and g == 0:
                        pe.wait_ge(hT_ev, NG * KT)
                    if at == 1 and g > 0:
                        pe.wait_ge(y_ev, g)
                    project_out(u - 1, start=(at == 1), stop=(at == 0))
                if par == 0:
                    project_values(p, g, 1)
                elif more:
                    project_values(p + 1, g + (at == H - 1), 0)

            project(0, 0)
            project_values(0, 0, 0)
            attention(pe, step)
            keep_warm(QB_, 8)
            pe.wait_ge(deq_ev, 2 * (PAIRS - 1))
            turn_diff(UNITS - 1)
            keep_warm(QB_, 4)
            attend(PAIRS - 1, UNITS - 1, 1)
            keep_warm(QB_, 7)
            project_out(UNITS - 1, start=False, stop=True)
            turn_weights(PAIRS - 1)
            keep_warm(QB_, 5)

            pe.wait_ge(gru_in, 16 * NGRU)
            pe.wait_ge(y_ev, NG)
            pe.wait_ge(deq_ev, 2 * PAIRS)

            def gates_in(c, part, i):
                g, k = i // KT, i % KT
                if i == 0:
                    pe.wait_ge(x_chunk_done, c + 1)
                    if part == 1 and not (isinstance(c, int) and c == 0):
                        pe.wait_ge(gates_ev, 2 * c + 1)
                    elif not (isinstance(c, int) and c <= 2):
                        pe.wait_ge(tr_ev, c - 2)
                n0 = (2 * part + g) * D
                last = pe.matmul(bank[gates_bank(c, part)][:, g * D:(g + 1) * D], x_chunk[:, k, :], wih[:, k, n0:n0 + D],
                                 start=(k == 0), stop=(k == KT - 1))
                if i == PIECES["in", part] - 1:
                    last.then_inc(gates_mm, 1)

            def recur(t, s):
                w = whh.rearrange("p k (g f) -> p k g f", g=3)
                for b, at, own, preset, done in ((RN_, FQ, slice(0, 3, 2), preset_rn, rn_mm),
                                                 (Z_, 0, slice(1, 2), preset_z, z_mm)):
                    pe.wait_ge(preset, t + 1)
                    n = len(range(3)[own]) * FQ
                    for k in range(KT):
                        if b == RN_:
                            pe.wait_ge(h_ready, KT * t + (k + 1))
                        for j in range(NQD):
                            last = pe.matmul(bank[b][j * QD:(j + 1) * QD, at:at + n], ring[:, (s - 1) % STEPS, k, :],
                                             w[:, k, own, j * FQ:(j + 1) * FQ], start=False, stop=(k == KT - 1),
                                             skip_group_check=True, tile_position=(0, j * QD))
                    last.then_inc(done, 1)

            def hidden(f, j, i, up):
                n, k = i // KT, i % KT
                if i == 0 and j == 0 and not up:
                    pe.wait_ge(hchunk_done, f + 1)
                if i == 0 and not up and not (isinstance(f, int) and f == 0 and j < 2):
                    pe.wait_ge(inter_done, f * MJ + (j - 1))
                dst = bank[(UP_ if up else GATE_)[j % 2]]
                m = NJ * j + n
                last = pe.matmul(dst[:, n * TOK:(n + 1) * TOK], wguT[:, (KT if up else 0) + k, m * P:(m + 1) * P],
                                 hchunk[:, k, :], start=(k == 0), stop=(k == KT - 1))
                if i == NJ * KT - 1:
                    last.then_inc(up_mm if up else gate_mm, 1)

            def down(f, j, i):
                n, o = i // KT, i % KT
                if i == 0:
                    pe.wait_ge(inter_done, f * MJ + (j + 1))
                    if j == 0 and not (isinstance(f, int) and f == 0):
                        pe.wait_ge(fin_done, f)
                m = NJ * j + n
                last = pe.matmul(bank[DOWN_][:, o * TOK:(o + 1) * TOK], wdT[:, m, o * P:(o + 1) * P],
                                 inter[j % 2][:, n * TOK:(n + 1) * TOK], start=(m == 0 and o == 0),
                                 stop=(m == MT - 1), skip_group_check=True)
                if i == NJ * KT - 1:
                    last.then_inc(down_mm, 1)

            def turn_out(f):
                pe.wait_ge(fin_done, f + 1)
                if not (isinstance(f, int) and f >= CHUNKS - 2):
                    pe.wait_ge(gates_ev, 2 * f + 6)
                else:
                    pe.wait_ge(tr_ev, f)
                for o in range(KT):
                    last = pe.transpose(bank[TR_][:, o * P:(o + 1) * P],
                                        fin[:, o, :, :].rearrange("p b t -> p (b t)"), ident[:, :])
                last.then_inc(tr_mm, 1)

            def chunk(c, gru, mlp, more, end):
                f = c - 1
                for s in range(STEPS):
                    if gru:
                        recur(c * STEPS + s, s)
                        if not mlp:
                            keep_warm(DOWN_, 3)
                    for kind, j, i in SLOTS[s]:
                        if kind == "in" and more:
                            gates_in(c + 1, j, i)
                        elif kind == "in" and mlp and gru:
                            pe.wait_ge(inter_done, f * MJ + 1)
                            keep_warm(UP_[0], 2)
                        if kind in ("gate", "up") and mlp:
                            hidden(f, j, i, kind == "up")
                        if kind == "down" and mlp:
                            down(f, j, i)
                        if kind == "last" and end:
                            down(f - 1, j, i)
                        if kind == "turn" and end:
                            turn_out(f - 1)

            for part in range(2):
                for i in range(PIECES["in", part]):
                    gates_in(0, part, i)
            keep_warm(DOWN_, 20)
            chunks(pe, chunk)
            for i in range(NJ * KT):
                down(CHUNKS - 1, MJ - 1, i)
            turn_out(CHUNKS - 1)

        @block.scalar
        def _(act):
            act.dma_start(wk_c[:, :, :], Wk_c.rearrange("(k p) n -> p k n", p=P)).then_inc(wc_in, 16)
            act.dma_start(wo_c[:, :, :], Wo_c.rearrange("(k p) n -> p k n", p=P)).then_inc(wo_c_in, 16)
            act.dma_start(rmsw_b[:, :], rms_weight.rearrange("(a n) -> a n", a=1).broadcast_to([B * NBLK, D])).then_inc(row_in, 16)
            act.dma_start(query_b[:, :], cond[1:2, :].broadcast_to([B * NBLK, D])).then_inc(row_in, 16)
            act.dma_start(lam[:, :], lambda_init.rearrange("(a n) -> a n", a=1).broadcast_to([P, H])).then_inc(row_in, 16)
            with nc.allow_non_contiguous_dma(reason="two short vectors onto partitions"):
                act.dma_start(gamma[:, :], ln_gamma.rearrange("(k p) -> p k", p=P)).then_inc(ab_in, 16)
                act.dma_start(beta[:, :], ln_beta.rearrange("(k p) -> p k", p=P)).then_inc(ab_in, 16)

            act.preload_act_table(ACT.Sqrt)
            for w, b in ((wkT_c, 0), (woT_c, 1)):
                act.wait_ge(wcT_mm, b + 1)
                act.activation(w[:, :, :], cols(b, KT, D), ACT.Copy).then_inc(wcT_ev, 1)
            for i in range(NG * KT):
                g, k = i // KT, i % KT
                act.wait_ge(blocks_done, i + 1)
                act.activation(xT[:, k, g * GB:(g + 1) * GB, :], xT_bank(g, k)[:, :].rearrange("p (b t) -> p b t", b=GB),
                               ACT.Copy).then_inc(xT_ev, 1)
            act.wait_ge(dot_done, 1)
            act.activation(junk64a[:, :], bank[3][0:B * NBLK, 0:D], ACT.Square, accum_out=ssq[:, :]).then_inc(ssq_done, 1)
            act.wait_ge(ssq_done, 1)
            act.wait_ge(eps_set, 1)
            act.activation(rms[:, :], ssq[:, :], ACT.Sqrt, bias=eps[0:B * NBLK, :], scale=1.0 / D).then_inc(rms_done, 1)
            act.preload_act_table(ACT.Exp)
            act.wait_ge(rows_done, 1)
            act.activation(row_e[:, :, :], row_s[:, :, :], ACT.Exp).then_inc(rexp_done, 1)
            act.wait_ge(row_in, 16 * n_rows)
            act.activation(lam_e[:, :], lam[:, :], ACT.Exp, scale=-1.0).then_inc(lam_exp, 1)
            act.preload_act_table(ACT.Sqrt)
            act.wait_ge(consts, NCONST)
            act.activation(batch_of[:, :, :], batch_32, ACT.Copy).then_inc(batch_done, 1)
            def split_weights(p, par):
                act.wait_ge(wqk_in[par], p * 32 + 32)
                act.activation(w_hi[:, :, :, :], wqk[par][:, :, :, :], ACT.Copy).then_inc(w_hi_done, 1)

            def split_value_weights(p):
                act.wait_ge(wv_in, p * 16 + 16)
                act.activation(wv_hi[:, :, :], wv[:, :, :], ACT.Copy).then_inc(wv_hi_done, 1)

            split_weights(0, 0)
            split_value_weights(0)
            act.wait_ge(proj_mm, 1)
            act.activation(proj_hi[:, :], bank[1][0:B, 0:D], ACT.Copy).then_inc(proj_hi_done, 1)
            act.wait_ge(ab_in, 32)

            def norm_root(g):
                own = slice(g * GB, (g + 1) * GB)
                act.wait_ge(var_done, g + 1)
                act.activation(std[:, own], meanvar[:, own, 1], ACT.Sqrt, bias=eps[:, :]).then_inc(std_done, 1)

            def norm_out(g):
                act.wait_ge(hT_mm, g + 1)
                for k in range(KT):
                    for dst in (h_hi[:, g, k, :], hT[:, k, g * W4:(g + 1) * W4]):
                        last = act.activation(dst, hT_bank(g, k)[:, :], ACT.Identity, bias=beta[:, k:k + 1],
                                              scale=gamma[:, k:k + 1])
                    last.then_inc(hT_ev, 1)

            norm_root(0)
            norm_out(0)

            def queries_keys(p, u, par, last):
                act.wait_ge(q_mm, u + 1)
                act.activation(qT[:, :], bank[QB_][:, :], ACT.Copy, scale=SCALE).then_inc(q_ev, 1)
                act.wait_ge(k_mm, u + 1)
                act.activation(kT[:, :], bank[KB_][:, :], ACT.Copy).then_inc(k_ev, 1)
                if not last:
                    split_weights(p + par, 1 - par)

            def outputs(u):
                act.wait_ge(o_mm, u + 1)
                act.activation(att_hi[:, :], bank[TO_][:, :], ACT.Copy).then_inc(o_hi, 1)

            def values_first(p, i):
                act.wait_ge(v_mm, p * 2 + 1)
                last = act.activation(v[:, i, 0:2, :], cols(VB_, 4, HD)[:, i::2, :], ACT.Copy)
                if i == 1:
                    last.then_inc(v_ev, 1)

            def values_second(p):
                act.wait_ge(v_mm, p * 2 + 2)
                act.activation(v[:, :, 2:4, :].rearrange("p i b d -> p b i d"),
                               bank[VB_][:, :].rearrange("p (b i d) -> p b i d", b=2, i=2), ACT.Copy).then_inc(v_ev, 1)

            def keep_weights(p, part):
                act.wait_ge(deq_mm, 2 * p + (part + 1))
                dst, src = ((wdT[:, bass.ds(p, 1), :].rearrange("p a d -> p (a d)"), bank[VB_][:, 0:D]),
                            (wguT[:, :, bass.ds(p * P, P)], cols(TO_, 2 * KT, P)))[part]
                act.activation(dst, src, ACT.Copy).then_inc(deq_ev, 1)

            def step(p, u, par, g):
                begun = not (isinstance(u, int) and u == 0)
                more = not (isinstance(u, int) and u == UNITS - 1)
                if begun:
                    outputs(u - 1)
                if par == 0:
                    values_first(p, 1)
                if begun:
                    act.wait_ge(diff_done, 2 * u)
                for i in range(2):
                    act.wait_ge(max_done, 2 * u + (i + 1))
                    for b in range(GB):
                        last = act.activation(exps[:, i, b, :], bank[SB_[i]][:, b * T:(b + 1) * T], ACT.Exp,
                                              bias=neg_max[:, i, b:b + 1], scale=1.0,
                                              accum_out=sums[:, i, b:b + 1])
                    last.then_inc(exp_done, 1)
                if par == 0 and not (isinstance(p, int) and p == 0):
                    for part in range(2):
                        keep_weights(p - 1, part)
                if more:
                    queries_keys(p + par, u + 1, 1 - par, isinstance(u, int) and u == UNITS - 2)
                act.wait_ge(wo_in[par], (u - par) * 8 + 16)
                if begun:
                    act.wait_ge(wo_mm, u)
                act.activation(wo_hi[:, :], wo[par][:, :], ACT.Copy).then_inc(wo_hi_done, 1)
                if par == 0:
                    values_second(p)
                    if not (isinstance(p, int) and p == PAIRS - 1):
                        split_value_weights(p + 1)
                elif more:
                    values_first(p + 1, 0)
                act.wait_ge(t_mm, u + 1)
                act.activation(diffT[:, :], bank[TO_][:, :], ACT.Copy).then_inc(t_ev, 1)
                if isinstance(u, int) and u == 0:
                    norm_out(1)

            queries_keys(0, 0, 0, False)
            norm_root(1)
            act.preload_act_table(ACT.Exp)
            values_first(0, 0)
            attention(act, step)
            outputs(UNITS - 1)
            for part in range(2):
                keep_weights(PAIRS - 1, part)

            def preset(s):
                act.activation(bank[RN_][:, 0:3 * FQ], gates[:, s, FQ:4 * FQ], ACT.Copy).then_inc(preset_rn, 1)
                act.activation(bank[Z_][:, 0:FQ], gates[:, s, 0:FQ], ACT.Copy).then_inc(preset_z, 1)

            act.preload_act_table(ACT.Sigmoid)
            act.wait_ge(y_ev, NG)
            act.wait_ge(half_in[0], 16 * NQD)
            preset(0)

            def chunk(c, gru, mlp, more, end):
                f = c - 1
                if mlp:
                    act.wait_ge(h_ready, c * (KT * STEPS) + KT)
                    if not (isinstance(f, int) and f == 0):
                        act.wait_ge(up_mm, f * MJ)
                    act.activation(hchunk.rearrange("p k (t b) -> p t k b", b=B), ring[:, :, :, 0:B],
                                   ACT.Copy).then_inc(hchunk_done, 1)
                for s in range(STEPS):
                    if gru:
                        t = c * STEPS + s
                        after = s < STEPS - 1 or more
                        act.wait_ge(rn_mm, t + 1)
                        act.activation(r_g[:, :], bank[RN_][:, FQ:2 * FQ], ACT.Sigmoid).then_inc(r_act, 1)
                        act.wait_ge(z_mm, t + 1)
                        act.activation(z_g[:, :], bank[Z_][:, 0:FQ], ACT.Sigmoid).then_inc(z_act, 1)
                        act.activation(z_comp[:, :], bank[Z_][:, 0:FQ], ACT.Sigmoid, scale=-1.0).then_inc(z_act, 1)
                        for k in range(KT):
                            own = slice(k * QD, (k + 1) * QD)
                            act.wait_ge(npre_done, 2 * t + (k + 1))
                            act.activation(n_g[:, own], n_pre[:, own], ACT.Tanh).then_inc(n_act, 1)
                        if after:
                            if s == HALF - 1:
                                act.wait_ge(half_in[1], (c + 1) * (16 * NQD))
                            elif s == STEPS - 1:
                                act.wait_ge(half_in[0], (c + 2) * (16 * NQD))
                            act.wait_ge(z_act, 2 * t + 2)
                            preset((s + 1) % STEPS)
                    if mlp:
                        for j in range(MJ):
                            if s == TANH_AT[j]:
                                act.wait_ge(arg_done, f * MJ + (j + 1))
                                if not (isinstance(f, int) and f == 0 and j == 0):
                                    act.wait_ge(lin_done, f * MJ + j)
                                act.activation(g_tanh, g_arg, ACT.Tanh, scale=GELU_C * GELU_A).then_inc(tanh_done, 1)
                            if s == SQUARE_AT[j]:
                                act.wait_ge(gate_mm, f * MJ + (j + 1))
                                if not (isinstance(f, int) and f == 0 and j == 0):
                                    act.wait_ge(arg_done, f * MJ + j)
                                act.activation(g_sq, bank[GATE_[j % 2]][:, :], ACT.Square).then_inc(sq_done, 1)
                    if s == ROWS_AT and end:
                        rows_out(c - 2)

            def rows_out(f):
                act.wait_ge(tr_mm, f + 1)
                if not (isinstance(f, int) and f == 0):
                    act.wait_ge(stored, 16 * f)
                act.activation(out_sb[:, :], bank[TR_][:, 0:D], ACT.Copy).then_inc(tr_ev, 1)

            chunks(act, chunk)
            rows_out(CHUNKS - 1)

        @block.vector
        def _(dve):
            mark = [0]

            def then(ins):
                mark[0] += 1
                ins.then_inc(dve1, 1)
                dve.wait_ge(dve1, mark[0])

            for i in range(NG * KT):
                g, k = i // KT, i % KT
                dve.wait_ge(xT_mm, i + 1)
                dve.tensor_reduce(blocksT[:, k, g * GB * NBLK:(g + 1) * GB * NBLK],
                                  xT_bank(g, k)[:, :].rearrange("p (n t) -> p n t", t=BLK), AX, ALU.add).then_inc(blocks_done, 1)
            dve.wait_ge(row_in, 16 * n_rows)
            then(dve.tensor_tensor(wquery[:, :], rmsw_b[:, :], query_b[:, :], ALU.mult))
            dve.wait_ge(keys_mm, 1)
            dve.scalar_tensor_tensor(out=junk64[:, :], in0=bank[3][0:B * NBLK, 0:D], scalar=1.0, in1=wquery[:, :],
                                     op0=ALU.mult, op1=ALU.mult, accum_out=dot[:, :]).then_inc(dot_done, 1)
            dve.wait_ge(rms_done, 1)
            then(dve.reciprocal(rrms[:, :], rms[:, :]))
            dve.tensor_tensor(score_c[:, :], dot[:, :], rrms[:, :], ALU.mult).then_inc(score_done, 1)
            dve.wait_ge(score_mm, 1)
            row = bank[3][0:1, 256:256 + B * NBLK].rearrange("p (b n) -> p b n", b=B)
            then(dve.tensor_reduce(row_max[:, :], row, AX, ALU.max))
            dve.tensor_tensor(row_s[:, :, :], row, row_max[:, :].unsqueeze(2).broadcast_to([1, B, NBLK]),
                              ALU.subtract).then_inc(rows_done, 1)
            dve.wait_ge(rexp_done, 1)
            then(dve.tensor_reduce(row_sum[:, :], row_e[:, :, :], AX, ALU.add))
            then(dve.reciprocal(row_r[:, :], row_sum[:, :]))
            dve.tensor_tensor(row_p[:, :, :], row_e[:, :, :], row_r[:, :].unsqueeze(2).broadcast_to([1, B, NBLK]),
                              ALU.mult).then_inc(probs_done, 1)
            dve.wait_ge(bcast_mm, 1)
            then(dve.tensor_tensor(weighted[:, :, :], blocksT[:, :, :],
                                   bank[0][:, 0:B * NBLK].unsqueeze(1).broadcast_to([P, KT, B * NBLK]), ALU.mult))
            dve.tensor_reduce(attendedT[:, :, :], weighted.rearrange("p k (b n) -> p k b n", b=B), AX,
                              ALU.add).then_inc(att_done, 1)
            dve.wait_ge(proj_mm, 1)
            dve.wait_ge(proj_hi_done, 1)
            dve.tensor_tensor(proj_lo[:, :], bank[1][0:B, 0:D], proj_hi[:, :].bitcast(F32), ALU.subtract).then_inc(proj_ev, 1)

            def layer_norm(g):
                own = range(g * GB, (g + 1) * GB)
                for i in range(g * GB // 2, (g + 1) * GB // 2):
                    dve.wait_ge(projb_mm, i + 1)
                    last = dve.tensor_tensor(xn[:, 2 * i:2 * i + 2, :], x_sb[:, 2 * i:2 * i + 2, :], cols(4 + i, 2, D), ALU.add)
                then(last)
                for b in own:
                    last = dve.bn_stats(stats[:, b, :], xn[:, b, :])
                then(last)
                for b in own:
                    last = dve.bn_aggr(meanvar[:, b, :], stats[:, b, :])
                last.then_inc(var_done, 1)
                dve.wait_ge(std_done, g + 1)
                then(dve.reciprocal(rstd[:, g * GB:(g + 1) * GB], std[:, g * GB:(g + 1) * GB]))
                for b in own:
                    dve.tensor_scalar(xn[:, b, :], xn[:, b, :], meanvar[:, b, 0:1], rstd[:, b:b + 1], ALU.subtract,
                                      ALU.mult).then_inc(xn_done, 1)

            def norm_rest(g):
                for k in range(KT):
                    dve.wait_ge(hT_ev, g * KT + k + 1)
                    dve.tensor_tensor(h_lo[:, g, k, :], hT[:, k, g * W4:(g + 1) * W4], h_hi[:, g, k, :].bitcast(F32),
                                      ALU.subtract).then_inc(h_lo_done, 1)

            layer_norm(0)
            norm_rest(0)
            layer_norm(1)
            dve.wait_ge(lam_exp, 1)
            then(dve.tensor_scalar(lam_1[:, :], lam_e[:, :], 1.0, None, ALU.add))
            then(dve.reciprocal(lam_r[:, :], lam_1[:, :]))
            then(dve.tensor_scalar(neg_lam[:, :], lam_r[:, :], -1.0, None, ALU.mult))

            def codes(p):
                dve.wait_ge(packed_in, p * 48 + 48)
                src = packed.rearrange("p a n -> p (a n)")
                dve.tensor_scalar(code[:, :, 0], src, 7, None, ALU.bitwise_and).then_inc(bits_done, 1)
                dve.tensor_scalar(code[:, :, 1], src, 4, 7, ALU.logical_shift_right, ALU.bitwise_and).then_inc(bits_done, 1)
                dve.tensor_scalar(sign[:, :, 0], src, 8, 28, ALU.bitwise_and, ALU.logical_shift_left).then_inc(bits_done, 1)
                dve.tensor_scalar(sign[:, :, 1], src, 128, 24, ALU.bitwise_and, ALU.logical_shift_left).then_inc(bits_done, 1)

            def magnitudes(p):
                dve.wait_ge(bits_done, 4 * p + 4)
                dve.tensor_scalar(line2[:, :, :], code[:, :, :], 1.0, -2.0, ALU.mult, ALU.add).then_inc(lines_done, 1)
                dve.tensor_scalar(line3[:, :, :], code[:, :, :], 2.0, -8.0, ALU.mult, ALU.add).then_inc(lines_done, 1)
                dve.wait_ge(lines_done, 2 * p + 2)
                dve.scalar_tensor_tensor(out=mag[:, :, :], in0=code[:, :, :], scalar=0.5, in1=line2[:, :, :],
                                         op0=ALU.mult, op1=ALU.max).then_inc(mag_done, 1)
                dve.wait_ge(mag_done, 2 * p + 1)
                dve.tensor_tensor(mag[:, :, :], mag[:, :, :], line3[:, :, :], ALU.max).then_inc(mag_done, 1)

            def weights(p):
                dve.wait_ge(mag_done, 2 * p + 2)
                dve.tensor_tensor(value[:, :, :].bitcast(I32), mag[:, :, :].bitcast(I32), sign[:, :, :],
                                  ALU.bitwise_or).then_inc(value_done, 1)
                dve.wait_ge(value_done, p + 1)
                if not (isinstance(p, int) and p == 0):
                    dve.wait_ge(deq_mm, 2 * p)
                dve.wait_ge(scales_in, p * 48 + 48)
                blocks = value.rearrange("p (n q) i -> p n (q i)", n=NQ)
                scale = scales[:, :].unsqueeze(2).broadcast_to([P, NQ, QB])
                nb = D // QB
                for a in range(2):
                    own = slice(a * nb, (a + 1) * nb)
                    dve.tensor_tensor(wscaled[:, own, :].rearrange("p (k j) q -> p j k q", k=KT),
                                      blocks[:, own, :].rearrange("p (j k) q -> p j k q", k=KT),
                                      scale[:, own, :].rearrange("p (j k) q -> p j k q", k=KT), ALU.mult)
                dve.tensor_tensor(wscaled[:, 2 * nb:, :], blocks[:, 2 * nb:, :], scale[:, 2 * nb:, :],
                                  ALU.mult).then_inc(wscaled_done, 1)

            def outputs(u):
                dve.wait_ge(o_hi, u + 1)
                dve.tensor_tensor(att_lo[:, :], bank[TO_][:, :], att_hi[:, :].bitcast(F32), ALU.subtract).then_inc(o_ev, 1)

            def step(p, u, par, g):
                h = u - g * H
                dve.wait_ge(s_mm, u + 1)
                if not (isinstance(u, int) and u == 0):
                    dve.wait_ge(exp_done, 2 * u)
                for i in range(2):
                    dve.tensor_reduce(neg_max[:, i, :], cols(SB_[i], GB, T), AX, ALU.max, negate=True).then_inc(max_done, 1)
                if not (isinstance(u, int) and u == 0):
                    outputs(u - 1)
                dve.wait_ge(exp_done, 2 * u + 1)
                dve.reciprocal(rsums[:, 0, :], sums[:, 0, :]).then_inc(rsum_done, 1)
                dve.wait_ge(rsum_done, 2 * u + 1)
                for b in range(GB):
                    dve.tensor_scalar(probs1[:, b, :], exps[:, 0, b, :], rsums[:, 0, b:b + 1], None, ALU.mult)
                dve.wait_ge(exp_done, 2 * u + 2)
                dve.reciprocal(rsums[:, 1, :], sums[:, 1, :]).then_inc(rsum_done, 1)
                dve.wait_ge(rsum_done, 2 * u + 2)
                dve.tensor_scalar(coef2[:, :], rsums[:, 1, :], neg_lam[:, bass.ds(h, 1)], None, ALU.mult).then_inc(coef_done, 1)
                dve.wait_ge(coef_done, u + 1)
                for b in range(GB):
                    last = dve.scalar_tensor_tensor(out=diff[:, b, :], in0=exps[:, 1, b, :], scalar=coef2[:, b:b + 1],
                                                    in1=probs1[:, b, :], op0=ALU.mult, op1=ALU.add)
                    if b % 2:
                        last.then_inc(diff_done, 1)
                if isinstance(u, int) and u == H:
                    residual(0)
                if par == 0:
                    magnitudes(p)
                else:
                    weights(p)
                    if not (isinstance(p, int) and p == PAIRS - 1):
                        codes(p + 1)
                if isinstance(u, int) and u == 1:
                    norm_rest(1)

            def residual(g):
                dve.wait_ge(wo_mm, (g + 1) * H)
                for k in range(KT):
                    last = dve.tensor_tensor(x2T[:, k, :, g * GB:(g + 1) * GB].rearrange("p t b -> p b t"),
                                             cols(YB_[k], GB, T), xT[:, k, g * GB:(g + 1) * GB, :], ALU.add)
                last.then_inc(y_ev, 1)

            codes(0)
            attention(dve, step)
            outputs(UNITS - 1)
            dve.wait_ge(gru_in, 16 * NGRU)
            then(dve.tensor_tensor(gate_bias[:, 0:2 * D], gate_bias[:, 0:2 * D], bias_h[:, :], ALU.add))
            dve.transpose(ring[:, STEPS - 1, :, :].rearrange("p k q -> p (k q)"), h_row[:, :]).then_inc(h_ready, KT)
            residual(1)

            def tokens(c):
                if not (isinstance(c, int) and c == 0):
                    dve.wait_ge(gates_mm, 2 * c)
                for half in range(2):
                    last = dve.tensor_copy(
                        x_chunk[:, :, half * HALF * B:(half + 1) * HALF * B].rearrange("p k (b t) -> p k b t", b=B),
                        x2T[:, :, bass.ds(c * STEPS + half * HALF, HALF), :].rearrange("p k t b -> p k b t"))
                last.then_inc(x_chunk_done, 1)

            def gates_out(c, part):
                if part == 0 and not (isinstance(c, int) and c == 0):
                    for half in range(2):
                        dve.wait_ge(half_in[half], c * (16 * NQD))
                dve.wait_ge(gates_mm, 2 * c + (part + 1))
                g0, g1 = ((0, 2), (2, 3))[part]
                dst = gates_next.rearrange("p j (g f) -> p g j f", g=3)
                for g in range(g0, g1):
                    last = dve.tensor_tensor(dst[:, (g + 2) % 3, :, :],
                                             bank[gates_bank(c, part)][:, (g - g0) * D:(g - g0 + 1) * D].rearrange("p (j f) -> p j f", j=NQD),
                                             gate_bias[:, g * D:(g + 1) * D].rearrange("p (j f) -> p j f", j=NQD), ALU.add)
                last.then_inc(gates_ev, 1)

            dve.wait_ge(y_ev, NG)
            tokens(0)
            gates_out(0, 0)
            gates_out(0, 1)

            def chunk(c, gru, mlp, more, end):
                f = c - 1
                for s in range(STEPS):
                    if gru:
                        t = c * STEPS + s
                        half = [slice(k * QD, (k + 1) * QD) for k in range(KT)]
                        dve.wait_ge(r_act, t + 1)
                        for own in half:
                            dve.tensor_tensor(r_hn[:, own], bank[RN_][:, 2 * FQ:3 * FQ][:, own], r_g[:, own],
                                              ALU.mult).then_inc(rhn_done, 1)
                        for k, own in enumerate(half):
                            dve.wait_ge(rhn_done, 2 * t + (k + 1))
                            dve.tensor_tensor(n_pre[:, own], bank[RN_][:, own], r_hn[:, own], ALU.add).then_inc(npre_done, 1)
                        dve.wait_ge(z_act, 2 * t + 1)
                        dve.tensor_tensor(zh[:, :], z_g[:, :], h_row[:, :], ALU.mult)
                        for k, own in enumerate(half):
                            dve.wait_ge(n_act, 2 * t + (k + 1))
                            dve.tensor_tensor(zn[:, own], z_comp[:, own], n_g[:, own], ALU.mult).then_inc(zn_done, 1)
                        for k, own in enumerate(half):
                            dve.wait_ge(zn_done, 2 * t + (k + 1))
                            dve.tensor_tensor(h_row[:, own], zn[:, own], zh[:, own], ALU.add).then_inc(hrow_done, 1)
                        if s == 0 and mlp:
                            dve.wait_ge(hchunk_done, f + 1)
                        for k, own in enumerate(half):
                            dve.wait_ge(hrow_done, 2 * t + (k + 1))
                            dve.transpose(ring[:, s, k, :], h_row[:, own]).then_inc(h_ready, 1)
                    if s == 1 and more:
                        tokens(c + 1)
                    if s == FINISH_AT and end:
                        finish(c - 2)
                    if mlp:
                        for j in range(MJ):
                            n = f * MJ + (j + 1)
                            if s == TANH_AT[j]:
                                if not (isinstance(f, int) and f == 0 and j == 0):
                                    dve.wait_ge(inter_done, n - 1)
                                dve.wait_ge(tanh_done, n)
                                dve.scalar_tensor_tensor(out=g_lin, in0=g_tanh, scalar=1.0,
                                                         in1=bank[GATE_[j % 2]][:, :],
                                                         op0=ALU.add, op1=ALU.mult).then_inc(lin_done, 1)
                            if s == INTER_AT[j]:
                                intermediate(f, j)
                            if s == SQUARE_AT[j]:
                                dve.wait_ge(sq_done, n)
                                dve.scalar_tensor_tensor(out=g_arg, in0=g_sq, scalar=1.0 / GELU_A,
                                                         in1=bank[GATE_[j % 2]][:, :], op0=ALU.add,
                                                         op1=ALU.mult).then_inc(arg_done, 1)
                    if s == INTER_AT[MJ - 1] - STEPS and end:
                        intermediate(f - 1, MJ - 1)
                    for part in range(2):
                        if s == GATES_AT[part] and more:
                            gates_out(c + 1, part)

            def intermediate(f, j):
                n = f * MJ + (j + 1)
                dve.wait_ge(lin_done, n)
                dve.wait_ge(up_mm, n)
                if not (isinstance(f, int) and f == 0 and j < 2):
                    dve.wait_ge(down_mm, f * MJ + (j - 1))
                dve.scalar_tensor_tensor(out=inter[j % 2], in0=g_lin, scalar=0.5, in1=bank[UP_[j % 2]][:, :],
                                         op0=ALU.mult, op1=ALU.mult).then_inc(inter_done, 1)

            def finish(f):
                dve.wait_ge(down_mm, f * MJ + MJ)
                if not (isinstance(f, int) and f == 0):
                    dve.wait_ge(tr_mm, f)
                for o in range(KT):
                    last = dve.tensor_tensor(fin[:, o, :, :].rearrange("p b t -> p t b"),
                                             bank[DOWN_][:, o * TOK:(o + 1) * TOK].rearrange("p (t b) -> p t b", b=B),
                                             x2T[:, o, bass.ds(f * STEPS, STEPS), :], ALU.add)
                last.then_inc(fin_done, 1)

            chunks(dve, chunk)
            intermediate(CHUNKS - 1, MJ - 1)
            finish(CHUNKS - 1)


_INS = ['x', 'cond_2048', 'L0_cond_rms_weight', 'L0_cond_Wk', 'L0_cond_Wo', 'L0_cond_ln_gamma', 'L0_cond_ln_beta',
        'L0_attn_Wq', 'L0_attn_Wk', 'L0_attn_Wv', 'L0_attn_Wo', 'L0_attn_lambda_init',
        'L0_cond2_W_ih', 'L0_cond2_W_hh', 'L0_cond2_b_ih', 'L0_cond2_b_hh',
        'L0_ffn_gate_W_packed', 'L0_ffn_gate_scales', 'L0_ffn_up_W_packed', 'L0_ffn_up_scales',
        'L0_ffn_down_W_packed', 'L0_ffn_down_scales']
_OUTS = [((8, 128, 256), 'float32')]


def kernel(**inputs):
    import numpy as _np
    import concourse.bacc as _bacc
    from concourse import mybir as _mybir
    from concourse.bass_utils import run_bass_kernel_spmd as _run

    nc = _bacc.Bacc("TRN2", target_bir_lowering=False, num_devices=1)
    arrays, args = {}, []
    for name in _INS:
        a = _np.ascontiguousarray(inputs[name])
        arrays[f"in_{name}_dram"] = a
        args.append(nc.dram_tensor(f"in_{name}_dram", a.shape, _mybir.dt.from_np(a.dtype), kind="ExternalInput").ap())
    for i, (shape, dtype) in enumerate(_OUTS):
        dt = _mybir.dt.from_np(_np.dtype(dtype))
        args.append(nc.dram_tensor(f"out_{i}_dram", shape, dt, kind="ExternalOutput").ap())
    build(nc, *args)
    r = _run(nc, [arrays], core_ids=[0])
    got = tuple(r.results[0][f"out_{i}_dram"] for i in range(len(_OUTS)))
    return got[0]
```
